# Optimizing a Trainium2 kernel written in Bass

```python
import numpy as np
import jax
import jax.numpy as jnp

def _softmax(x, axis=-1):
    return jax.nn.softmax(x, axis=axis)

def _gelu(x):
    return jax.nn.gelu(x, approximate=True)

def _silu(x):
    return jax.nn.silu(x)

def _sigmoid(x):
    return jax.nn.sigmoid(x)

def _layernorm(x, axis=-1, eps=1e-05):
    m = jnp.mean(x, axis=axis, keepdims=True)
    v = jnp.var(x, axis=axis, keepdims=True)
    return (x - m) / jnp.sqrt(v + eps)

def _scatter_add(tgt, idx, src, axis=0):
    return tgt.at[idx].add(src)

def _segment_sum(src, seg, n):
    return jax.ops.segment_sum(src, seg, n)
kernel_name = 'mk_flamingo_gated_d1_seqx_r2_066b34'

def setup_inputs(seed: int=0):
    np.random.seed(seed)
    _w = jnp.asarray

    def _rec_inputs():
        import jax
        import jax.numpy as jnp
        _rk = jax.random.key(seed)
        x = -0.0002928 + 1 * jax.random.normal(jax.random.fold_in(_rk, 1), (8, 512, 512), jnp.float32)
        _lenS = 512 - jax.random.randint(jax.random.fold_in(_rk, 7), (8,), 0, max(1, 512 // 4) + 1, jnp.int32)
        _lenS2 = 512 - jax.random.randint(jax.random.fold_in(_rk, 8), (8,), 0, max(1, 512 // 4) + 1, jnp.int32)
        _ctx_1024P = jax.random.normal(jax.random.fold_in(_rk, 11), (8, 16, 512), jnp.float32)
        _ctx_1024c = jax.random.dirichlet(jax.random.fold_in(_rk, 511), 0.3 * jnp.ones((16,), jnp.float32), (8, 512))
        _ctx_1024t = jnp.einsum('bsk,bkd->bsd', _ctx_1024c, _ctx_1024P)
        _ctx_1024t = _ctx_1024t * jax.lax.rsqrt(jnp.mean(jnp.square(_ctx_1024t)) + 1e-12) * 0.953939
        ctx_1024 = -1.39393e-06 + 0.999914 * (_ctx_1024t + 0.3 * jax.random.normal(jax.random.fold_in(_rk, 611), (8, 512, 512), jnp.float32))
        _g = jax.random.normal(jax.random.fold_in(_rk, 9001), (2, 1), jnp.float32)
        _g = jnp.sign(_g) * jnp.maximum(jnp.abs(_g), 1.0) + (_g == 0) * 1.0
        g_xattn = _g[0]
        g_ffn = _g[1]
        return (x, ctx_1024, g_xattn, g_ffn)
    x, ctx_1024, g_xattn, g_ffn = _rec_inputs()

    def _L0_xattn_setup():
        import jax, jax.numpy as jnp
        import numpy as np
        EMB = 512
        HEADS = 16
        HEAD_DIM = EMB // HEADS
        key = jax.random.key(seed)
        ks = jax.random.split(key, 11)
        B, S = (2, 1024)
        scale = 1.0 / np.sqrt(EMB)
        inp = {'query': jax.random.normal(ks[0], (B, S, EMB), jnp.float32), 'key': jax.random.normal(ks[1], (B, S, EMB), jnp.float32), 'value': jax.random.normal(ks[2], (B, S, EMB), jnp.float32), 'Wq': jax.random.normal(ks[3], (EMB, EMB), jnp.float32) * scale, 'bq': jnp.zeros((EMB,), jnp.float32), 'Wk': jax.random.normal(ks[4], (EMB, EMB), jnp.float32) * scale, 'bk': jnp.zeros((EMB,), jnp.float32), 'Wv': jax.random.normal(ks[5], (EMB, EMB), jnp.float32) * scale, 'bv': jnp.zeros((EMB,), jnp.float32), 'Wo': jax.random.normal(ks[6], (EMB, EMB), jnp.float32) * scale, 'bo': jnp.zeros((EMB,), jnp.float32)}
        return inp
    _L0_xattn_all = _L0_xattn_setup()
    _L0_xattn_in = {k: v for k, v in _L0_xattn_all.items() if k in ('Wq', 'bq', 'Wk', 'bk', 'Wv', 'bv', 'Wo', 'bo')}
    del _L0_xattn_all

    def _L0_ffn_setup():
        import jax, jax.numpy as jnp
        import numpy as np
        B, S, H, E = (4, 1024, 512, 8)
        key = jax.random.key(seed)
        k1, k2, k3 = jax.random.split(key, 3)
        scale_w = 1.0 / np.sqrt(H)
        return {'x': jax.random.normal(k1, (B, S, H), dtype=jnp.float32), 'router_w': jax.random.normal(k2, (H, E), dtype=jnp.float32) * scale_w, 'router_b': jnp.zeros((E,), dtype=jnp.float32), 'expert_w': jax.random.normal(k3, (E, H, H), dtype=jnp.float32) * scale_w, 'expert_b': jnp.zeros((E, H), dtype=jnp.float32)}
    _L0_ffn_all = _L0_ffn_setup()
    _L0_ffn_in = {k: v for k, v in _L0_ffn_all.items() if k in ('router_w', 'router_b', 'expert_w', 'expert_b')}
    del _L0_ffn_all
    return {'x': x, 'ctx_1024': ctx_1024, 'g_xattn': g_xattn, 'g_ffn': g_ffn, 'L0_xattn_Wq': _L0_xattn_in['Wq'], 'L0_xattn_bq': _L0_xattn_in['bq'], 'L0_xattn_Wk': _L0_xattn_in['Wk'], 'L0_xattn_bk': _L0_xattn_in['bk'], 'L0_xattn_Wv': _L0_xattn_in['Wv'], 'L0_xattn_bv': _L0_xattn_in['bv'], 'L0_xattn_Wo': _L0_xattn_in['Wo'], 'L0_xattn_bo': _L0_xattn_in['bo'], 'L0_ffn_router_w': _L0_ffn_in['router_w'], 'L0_ffn_router_b': _L0_ffn_in['router_b'], 'L0_ffn_expert_w': _L0_ffn_in['expert_w'], 'L0_ffn_expert_b': _L0_ffn_in['expert_b']}

def reference(x, ctx_1024, g_xattn, g_ffn, L0_xattn_Wq, L0_xattn_bq, L0_xattn_Wk, L0_xattn_bk, L0_xattn_Wv, L0_xattn_bv, L0_xattn_Wo, L0_xattn_bo, L0_ffn_router_w, L0_ffn_router_b, L0_ffn_expert_w, L0_ffn_expert_b):
    import jax
    import jax.numpy as jnp

    def _L0_xattn_ref(query, key, value, Wq, bq, Wk, bk, Wv, bv, Wo, bo):
        import jax, jax.numpy as jnp
        import numpy as np
        EMB = 512
        HEADS = 16
        HEAD_DIM = EMB // HEADS
        B, S, _ = query.shape
        Q = query @ Wq.T + bq
        K = key @ Wk.T + bk
        V = value @ Wv.T + bv
        Q = Q.reshape(B, S, HEADS, HEAD_DIM).transpose(0, 2, 1, 3)
        K = K.reshape(B, S, HEADS, HEAD_DIM).transpose(0, 2, 1, 3)
        V = V.reshape(B, S, HEADS, HEAD_DIM).transpose(0, 2, 1, 3)
        scores = jnp.einsum('bhqd,bhkd->bhqk', Q, K) / jnp.sqrt(jnp.asarray(HEAD_DIM, Q.dtype))
        attn = jax.nn.softmax(scores, axis=-1)
        ctx = jnp.einsum('bhqk,bhkd->bhqd', attn, V)
        ctx = ctx.transpose(0, 2, 1, 3).reshape(B, S, EMB)
        return ctx @ Wo.T + bo

    def _L0_ffn_ref(x, router_w, router_b, expert_w, expert_b):
        import jax, jax.numpy as jnp
        import numpy as np
        B, S, H, E = (4, 1024, 512, 8)
        b, s, h = x.shape
        xt = x.reshape(b * s, h)
        logits = xt @ router_w + router_b
        probs = jax.nn.softmax(logits, axis=-1)
        gate = jnp.max(probs, axis=-1)
        idx = jnp.argmax(probs, axis=-1)
        out_all = jnp.einsum('th,ehd->ted', xt, expert_w) + expert_b[None, :, :]
        e_out = jnp.take_along_axis(out_all, idx[:, None, None], axis=1)[:, 0, :]
        y = gate[:, None] * e_out
        return y.reshape(b, s, h)
    x = x + jnp.tanh(g_xattn[0]) * _L0_xattn_ref(_layernorm(x, axis=-1), ctx_1024, ctx_1024, L0_xattn_Wq, L0_xattn_bq, L0_xattn_Wk, L0_xattn_bk, L0_xattn_Wv, L0_xattn_bv, L0_xattn_Wo, L0_xattn_bo)
    x = x + jnp.tanh(g_ffn[0]) * _L0_ffn_ref(_layernorm(x, axis=-1), L0_ffn_router_w, L0_ffn_router_b, L0_ffn_expert_w, L0_ffn_expert_b)
    return x

_drawn_inputs = setup_inputs


def setup_inputs(seed=0):
    import zlib

    import numpy as np

    out = dict(_drawn_inputs(seed))
    spreads = {'L0_xattn_bq': (0.0, 0.1),
     'L0_xattn_bk': (0.0, 0.1),
     'L0_xattn_bv': (0.0, 0.1),
     'L0_xattn_bo': (0.0, 0.1),
     'L0_ffn_router_b': (0.0, 0.1),
     'L0_ffn_expert_b': (0.0, 0.1)}
    factors = {}
    for name, (base, spread) in spreads.items():
        noise = np.random.default_rng([zlib.crc32(name.encode()), seed]).standard_normal(out[name].shape)
        drawn = base * np.exp(spread * noise) if base else spread * noise
        out[name] = jnp.asarray(drawn.astype(out[name].dtype))
    for name, factor in factors.items():
        out[name] = (out[name] * factor).astype(out[name].dtype)
    return out
```

```python
from contextlib import ExitStack

import concourse.bass as bass
from concourse import mybir

F32 = mybir.dt.float32
F32R = mybir.dt.float32r
BF16 = mybir.dt.bfloat16
I32 = mybir.dt.int32
U32 = mybir.dt.uint32
ALU = mybir.AluOpType
ACT = mybir.ActivationFunctionType
AX = mybir.AxisListType

B, S, D = 8, 512, 512
HEADS, HD = 16, 32
E = 8
P = 128
NT = S // P
NF = D // P
HG = P // HD
TOKENS = B * S
SCALE = 1.0 / float(HD) ** 0.5
EPS = 1e-5
ROW = D + 3
MAXROW = 3 * HD
TILES = 40

STEPS = [
    "A0 M0 OU V0 SUM M1 A1 M2 V1 M3 Q A2 NM M4 V2 K M5 A3 ST M6 V3 OP0 M7 A4 LR0 OP1 RT0 RL0 RS0 RC0 LR1 MT".split(),
    "A0 M0 OU RT1 SUM M1 A1 M2 RL1 M3 Q A2 M4 RS1 K RC1 M5 A3 ST T0 M6 T1 M7 A4 T2 OP2 T3 LR2 MT".split(),
    "A0 M0 OP3 NMP OU SUM M1 LX0 A1 M2 RT2 LX1 M3 NM A2 RL2 T4 M4 LX2 RS2 T5 M5 A3 RC2 LX3 T6 M6 T7 M7 Q A4 K ST LR3 MT".split(),
    "A0 M0 OU SUM M1 A1 M2 RT3 NM Q M3 A2 RL3 M4 M5 K A3 ST RS3 M6 M7 A4 RC3 MT".split(),
]
LOADS = ["R0", "R1", "C0", "C1", "C2", "R2", "C3", "R3", "X0", "X1", "X2", "X3"]
CONSUMER = {"R": ("OP", 0), "C": ("T", 0), "X": ("T", NT)}
NSLOT = 3


def slot_of(name):
    return LOADS.index(name) % NSLOT


def load_count(name):
    same = [x for x in LOADS if x[0] == name[0] and slot_of(x) == slot_of(name)]
    return len(same), same.index(name)


def wait(eng, sem, per, b, offset, alone=None):
    if isinstance(b, int):
        if per * b + offset > 0:
            eng.wait_ge(sem, per * b + offset)
    else:
        assert per + offset > 0
        value = b * per + offset
        if alone is not None:
            value = eng.snap(value)
            eng.wait_ge(alone, 1)
        eng.wait_ge(sem, value)


def tenant_before(name, first, last):
    loads = [m for m in LOADS if not (first and m[0] == "R") and not (last and m[0] != "R")]
    if name not in loads:
        return None, False
    earlier = [m for m in loads[:loads.index(name)] if slot_of(m) == slot_of(name)]
    return (earlier[-1] if earlier else None), True


def build(nc, x, ctx, g_xattn, g_ffn, wq, bq, wk, bk, wv, bv, wo, bo, rw, rb, ew, eb, out):
    rows_dram = nc.dram_tensor("rows", [TOKENS, ROW], F32, kind="Internal").ap()
    lists_dram = nc.dram_tensor("lists", [E * TOKENS, 1], F32, kind="Internal").ap()
    out_rows = out.rearrange("b s d -> (b s) d")
    with ExitStack() as keep:
        def kept(name, shape, dt=F32):
            return keep.enter_context(nc.sbuf_tensor(name, shape, dt))

        counts = kept("counts", [P, E])
        ident = kept("ident", [P, P])
        attention_part(nc, x, ctx, g_xattn, g_ffn, wq, bq, wk, bk, wv, bv, wo, bo, rw, rb,
                       rows_dram, lists_dram, counts, ident)
        expert_part(nc, ew, eb, rows_dram, lists_dram, counts, ident, out_rows)


def attention_part(nc, x, ctx, g_xattn, g_ffn, wq, bq, wk, bk, wv, bv, wo, bo, rw, rb, rows_dram, lists_dram,
                   counts, ident):
    with ExitStack() as es:
        def sb(name, shape, dt=F32):
            return es.enter_context(nc.sbuf_tensor(name, shape, dt))

        def ps(name, shape):
            return es.enter_context(nc.psum_tensor(name, shape, F32))

        def sem(name):
            return es.enter_context(nc.semaphore(name))

        w_hi = [sb(f"w{n}_hi", [P, NF, D], F32R) for n in "qkvo"]
        w_lo = [sb(f"w{n}_lo", [P, NF, D], F32R) for n in "qkvo"]
        c_hi = sb("c_hi", [P, NF, S], F32R)
        c_lo = sb("c_lo", [P, NF, S], F32R)
        xn_hi = sb("xn_hi", [P, NF, S], F32R)
        xn_lo = sb("xn_lo", [P, NF, S], F32R)
        q_stack = [sb(f"q_stack{i}", [P, HG * S], F32R) for i in range(2)]
        k_stack = [sb(f"k_stack{i}", [P, HG * S], F32R) for i in range(2)]
        qk_hi = sb("qk_hi", [P, 2, S], F32R)
        qk_lo = sb("qk_lo", [P, 2, S], F32R)
        values = sb("values", [P, NT, D])
        probs = sb("probs", [P, 2, HG, S])
        psum_keys = sb("psum_keys", [P, HG, S])
        heads_hi = sb("heads_hi", [P, NF, S], F32R)
        heads_lo = sb("heads_lo", [P, NF, S], F32R)
        heads_raw = sb("heads_raw", [P, S])
        recip = sb("recip", [P, S])
        stage = [sb(f"stage{i}", [P, D]) for i in range(NSLOT)]
        row = [sb(f"row{i}", [P, ROW]) for i in range(2)]
        x2 = sb("x2", [P, D])
        x2_t = sb("x2_t", [P, NF, P])
        gbo = sb("gbo", [P, D])
        part = sb("part", [P, P])
        rw_pad = sb("rw_pad", [P, NF, HD])
        sel = sb("sel", [P, E])
        ones = sb("ones", [P, HD])
        before = sb("before", [P, P], BF16)
        ones_b = sb("ones_b", [P, P], BF16)
        chosen = sb("chosen", [P, E], BF16)
        bias = sb("bias", [P, 3, NF])
        rb_all = sb("rb_all", [P, E])
        tiny = sb("tiny", [P, 8])
        g_all, tanh_g, minus_half, token = tiny[:, 0:2], tiny[:, 2:4], tiny[:, 4:5], tiny[:, 5:6]
        token_of = [tiny[:, 6:7], tiny[:, 7:8]]
        numbers = sb("numbers", [P, E])
        maxima = sb("maxima", [P, 16])
        max_parts = sb("max_parts", [P, 32], F32R)
        max_rows = sb("max_rows", [32, P], F32R)
        st1 = [sb(f"st1_{i}", [P, 12]) for i in range(2)]
        st2 = [sb(f"st2_{i}", [P, 12]) for i in range(2)]
        rt = sb("rt", [P, 72])
        dests = sb("dests", [P, 2], I32)
        dest = [dests[:, 0:1], dests[:, 1:2]]

        sc = ps("sc", [P, HG, S])
        mb = ps("mb", [P, 2, S])
        hb = ps("hb", [P, S])
        jb = ps("jb", [P, S])

        s = {n: sem(n) for n in (
            "began", "w_in", "empty", "c_in0", "c_in1", "w_mm", "w_hi_done", "w_lo_done", "p_const", "d_const", "p_init", "a_const",
            "st_done", "exp_done", "acc_done", "pv_done", "ms_done", "mx_done", "mc_done", "mc_chain", "mt_mm",
            "mt_copied", "max_rows_in", "sum_mm", "sum_used", "ou_done", "nm_chain", "nm_done",
            "qk_mm", "hi_done", "lo_done", "stacked", "v_mm", "v_done", "op_mm", "xb_done", "x1_done",
            "t_mm", "t_hi", "t_lo", "lx_chain", "lx_var", "lx_pow", "lx_done",
            "lr_chain", "lr_var", "lr_pow", "lr_done", "rt_mm", "rt_done", "rl_mm", "rl_done",
            "rs_mm", "rs_chain", "rs_done", "rs_exp", "oh_done", "rc_mm", "rc_chain", "rc_done", "row_out0", "row_out1", "listed0", "listed1")}
        by_slot = {key: sem(f"staged_{key[0]}_{key[1]}") for key in sorted({(n[0], slot_of(n)) for n in LOADS})}
        staged = {n: by_slot[n[0], slot_of(n)] for n in LOADS}
        nat = [probs[:, 0], probs[:, 1], psum_keys[:, :, :], values[:, :, :]]

        def wait_staged(eng, name, b):
            n, k = load_count(name)
            wait(eng, staged[name], 16 * n, b, 16 * (k + 1))

        def target(c):
            return (0, c + 2) if c < 2 else (1, c - 2)

        def skipped(item, c, first, last):
            kind = item.rstrip("0123456789")
            if first and kind in ("OP", "LR", "RT", "RL", "RS", "RC"):
                return True
            if first and c == 0 and kind in ("OU", "SUM", "NM"):
                return True
            if last and (kind in ("T", "LX") or (kind in ("Q", "K") and c >= 2) or (kind == "ST" and c >= 2) or
                         (kind in ("M", "MT") and c == 3)):
                return True
            return False

        def steps(b, first=False, last=False):
            for c in range(4):
                for item in STEPS[c]:
                    if not skipped(item, c, first, last):
                        kind = item.rstrip("0123456789")
                        yield c, kind, int(item[len(kind):] or 0)

        def all_batches(eng, body):
            body(0, first=True)
            with eng.Fori(1, B - 1) as b:
                body(b)
            body(B - 1, last=True)

        PROLOGUE = "T0 T1 T2 LX0 T3 LX1 T4 LX2 T5 LX3 T6 T7".split()
        EPILOGUE = "OU SUM NM OP0 LR0 OP1 RT0 RL0 RS0 RC0 LR1 RT1 RL1 RS1 RC1 OP2 LR2 OP3 RT2 RL2 RS2 RC2 LR3 RT3 RL3 RS3 RC3".split()

        def split(item):
            kind = item.rstrip("0123456789")
            return kind, int(item[len(kind):] or 0)

        block = es.enter_context(nc.Block())

        @block.sync
        def _(sp):
            for i, w in enumerate((wq, wk, wv, wo)):
                sp.dma_start(nat[i], w.rearrange("(c p) i -> p c i", p=P)).then_inc(s["w_in"], 16)
                sp.wait_ge(s["w_in"], 16 * (i + 1))
            sp.dma_start(rb_all[:], rb.partition_broadcast(P)).then_inc(s["row_out0"], 16)
            sp.dma_start(gbo[:], bo.partition_broadcast(P)).then_inc(s["row_out1"], 16)
            for i, v in enumerate((bq, bk, bv)):
                sp.dma_start(bias[:, i, :], v.rearrange("(c p) -> p c", p=P), allow_slow_non_contiguous=True).then_inc(s["c_in0"], 16)
            sp.dma_start(g_all[:, 0:1], g_xattn.partition_broadcast(P)).then_inc(s["c_in0"], 16)
            sp.dma_start(g_all[:, 1:2], g_ffn.partition_broadcast(P)).then_inc(s["c_in0"], 16)
            sp.wait_ge(s["d_const"], 1)
            sp.dma_start(rw_pad[:, :, 0:E], rw.rearrange("(c p) e -> p c e", p=P)).then_inc(s["c_in1"], 16)

            def load(name, b):
                kind, t = name[0], int(name[1])
                src, tb = {"R": (x, b - 1), "C": (ctx, b + 1), "X": (x, b + 1)}[kind]
                rows_of = src[tb, t * P:(t + 1) * P, :] if isinstance(tb, int) else \
                    src[bass.ds(tb, 1), t * P:(t + 1) * P, :].rearrange("a p d -> (a p) d")
                sp.dma_start(stage[slot_of(name)][:], rows_of).then_inc(staged[name], 16)

            def load_after(kind, n, b, first=False, last=False):
                for name in LOADS:
                    before, there = tenant_before(name, first, last)
                    if there and before and (CONSUMER[before[0]][0], CONSUMER[before[0]][1] + int(before[1])) == (kind, n):
                        if kind == "OP":
                            wait(sp, s["x1_done"], NT, b, -NT + n + 1, s["began"])
                        else:
                            wait(sp, s["t_mm"], 8, b, 8 + n + 1, s["began"])
                        load(name, b)

            def first_loads(b, first=False, last=False):
                wait(sp, s["t_mm"], 8, b, 8 if not isinstance(b, int) or b < B else 0, s["began"])
                for name in LOADS:
                    before, there = tenant_before(name, first, last)
                    if there and before is None:
                        load(name, b)

            def row_to_dram(n, b):
                wait(sp, s["rs_chain"], NT * 8, b, 8 * (n - NT) + 8, s["began"])
                tb = b - 1
                dst = rows_dram[(tb * NT + n) * P:(tb * NT + n + 1) * P, :] if isinstance(b, int) else \
                    rows_dram[bass.ds(tb * S + n * P, P), :]
                sp.dma_start(dst, row[n % 2][:, :]).then_inc(s[f"row_out{n % 2}"], 16)

            def stack(c, b, db):
                wait(sp, s["lo_done"], 8, b, 8 * db + 2 * c + 2, s["began"])
                wait(sp, s["st_done"], 32, b, 32 * db + 8 * (c - 1), s["began"])
                for h in range(HG):
                    cols, rows = slice(h * S, (h + 1) * S), slice(h * HD, (h + 1) * HD)
                    for i, stk, parts in ((0, q_stack, (qk_hi, qk_hi, qk_lo)), (1, k_stack, (qk_hi, qk_lo, qk_hi))):
                        for j, src in enumerate(parts):
                            sp.dma_start(stk[c % 2][j * HD:(j + 1) * HD, cols].bitcast(F32),
                                         src[rows, i, :].bitcast(F32)).then_inc(s["stacked"], 16)

            inputs = [name for name in LOADS if name[0] != "R"]
            for n, name in enumerate(inputs):
                earlier = [m for m in inputs[:n] if slot_of(m) == slot_of(name)]
                if earlier:
                    sp.wait_ge(s["t_mm"], (0 if earlier[-1][0] == "C" else NT) + int(earlier[-1][1]) + 1)
                load(name, -1)
            stack(0, 0, 0)
            stack(1, 0, 0)

            def body(b, first=False, last=False):
                first_loads(b, first, last)
                for c, kind, n in steps(b, first, last):
                    if kind in ("OP", "T"):
                        load_after(kind, n, b, first, last)
                    elif kind == "ST":
                        db, tc = target(c)
                        stack(tc, b, db)
                    elif kind == "RC":
                        row_to_dram(n, b)

            all_batches(nc.sync, body)
            first_loads(B, last=True)
            for it in EPILOGUE:
                kind, n = split(it)
                if kind == "OP":
                    load_after(kind, n, B, last=True)
                elif kind == "RC":
                    row_to_dram(n, B)
            for j in range(2):
                sp.wait_ge(s[f"row_out{j}"], 16 + 32 * B)

        @block.tensor
        def _(pe):
            def three(out_ap, a_hi, a_lo, b_hi, b_lo):
                last = None
                for i in range(NF):
                    for n, (a, m) in enumerate(((a_hi, b_hi), (a_lo, b_hi), (a_hi, b_lo))):
                        last = nc.tensor.matmul(out_ap, a(i), m(i), start=(i == 0 and n == 0),
                                                stop=(i == NF - 1 and n == 2))
                return last

            free = [None]

            def jb_free():
                if free[0] is not None:
                    wait(pe, *free[0])

            def jb_held(sem_, per, b, offset):
                free[0] = (sem_, per, b, offset)

            pe.wait_ge(s["p_const"], 2)
            pe.wait_ge(s["w_in"], 64)
            for n in range(4 * NF):
                i, k = n // NF, n % NF
                if n >= 4:
                    pe.wait_ge(s["w_lo_done"], n - 3)
                for o in range(NF):
                    last = nc.tensor.transpose(sc[:, n % 4, o * P:(o + 1) * P],
                                               nat[i][:, o, k * P:(k + 1) * P], ident[:])
                last.then_inc(s["w_mm"], 1)
            pe.wait_ge(s["w_lo_done"], 4 * NF)
            pe.wait_ge(s["p_init"], 2)
            pe.wait_ge(s["c_in1"], 16)

            def item(kind, n, c, b, db=0, last_group=False):
                u4 = 4 * db + c
                if kind == "A":
                    if n < NT:
                        if n == 0:
                            wait(pe, s["max_rows_in"], 128, b, 32 * (u4 + 1))
                        for h2 in range(2):
                            wait(pe, s["exp_done"], 32, b, 8 * u4 + 2 * n + h2 - 1)
                            for h in (2 * h2, 2 * h2 + 1):
                                last = nc.tensor.matmul(
                                    sc[:, h, :], k_stack[c % 2][0:MAXROW + 2, h * S + n * P:h * S + (n + 1) * P],
                                    q_stack[c % 2][0:MAXROW + 2, h * S:(h + 1) * S], start=True, stop=True)
                            last.then_inc(s["st_done"], 1)
                    if n >= 1:
                        kt = n - 1
                        if kt == 0:
                            wait(pe, s["ou_done"], 4, b, u4)
                        if c == 0:
                            wait(pe, s["v_done"], NT, b, NT * db + kt + 1)
                        wait(pe, s["exp_done"], 32, b, 8 * u4 + 2 * kt + 2)
                        for h in range(HG):
                            last = nc.tensor.matmul(
                                hb[h * HD:(h + 1) * HD, :], values[:, kt, (HG * c + h) * HD:(HG * c + h + 1) * HD],
                                probs[:, kt % 2, h, :], start=(kt == 0), stop=(kt == NT - 1))
                        last.then_inc(s["pv_done"], 1)
                elif kind == "M":
                    g = u4 + 1
                    if n == 0:
                        wait(pe, s["stacked"], 4 * 16 * 24, b, 16 * 24 * (g + 1))
                    wait(pe, s["mx_done"], 32, b, 8 * g + n)
                    h, st = n // 2, (c + 1) % 2
                    for j in range(2):
                        q0 = h * S + (2 * (n % 2) + j) * P
                        last = nc.tensor.matmul(mb[:, j, :], q_stack[st][0:MAXROW, q0:q0 + P],
                                                k_stack[st][0:MAXROW, h * S:(h + 1) * S], start=True, stop=True)
                    last.then_inc(s["ms_done"], 1)
                elif kind == "MT":
                    wait(pe, s["mc_done"], 4, b, u4 + 2)
                    jb_free()
                    nc.tensor.transpose(jb[0:32, 0:P], max_parts[:, :].bitcast(F32), ident[:]).then_inc(s["mt_mm"], 1)
                    jb_held(s["mt_copied"], 4, b, u4 + 2)
                elif kind == "SUM":
                    wait(pe, s["acc_done"], 24, b, 6 * (u4 - 1) + 6)
                    jb_free()
                    for h in range(HG):
                        last = nc.tensor.matmul(jb[h * HD:(h + 1) * HD, :], ones[:], psum_keys[:, h, :],
                                                start=True, stop=True)
                    last.then_inc(s["sum_mm"], 1)
                    jb_held(s["sum_used"], 4, b, u4)
                elif kind in ("Q", "K"):
                    i = 0 if kind == "Q" else 1
                    src_hi, src_lo = (xn_hi, xn_lo) if i == 0 else (c_hi, c_lo)
                    wait(pe, s["t_lo"], 8, b, 8 * (db + 1))
                    wait(pe, s["t_hi"], 8, b, 8 * (db + 1))
                    jb_free()
                    three(jb[:], lambda k: w_hi[i][:, k, c * P:(c + 1) * P], lambda k: w_lo[i][:, k, c * P:(c + 1) * P],
                          lambda k: src_hi[:, k, :], lambda k: src_lo[:, k, :]).then_inc(s["qk_mm"], 1)
                    jb_held(s["lo_done"], 8, b, 2 * u4 + i + 1)
                elif kind == "V":
                    jb_free()
                    three(jb[:], lambda k: c_hi[:, k, n * P:(n + 1) * P], lambda k: c_lo[:, k, n * P:(n + 1) * P],
                          lambda k: w_hi[2][:, k, :], lambda k: w_lo[2][:, k, :]).then_inc(s["v_mm"], 1)
                    jb_held(s["v_done"], NT, b, n + 1)
                elif kind == "OP":
                    wait(pe, s["nm_done"], 4, b, 0)
                    jb_free()
                    three(jb[:], lambda k: heads_hi[:, k, n * P:(n + 1) * P], lambda k: heads_lo[:, k, n * P:(n + 1) * P],
                          lambda k: w_hi[3][:, k, :], lambda k: w_lo[3][:, k, :]).then_inc(s["op_mm"], 1)
                    jb_held(s["x1_done"], NT, b, -NT + n + 1)
                elif kind == "T":
                    name = ("C" if n < NT else "X") + str(n % NT)
                    if n < NT:
                        wait_staged_pe(name, b, db - 1)
                    else:
                        wait(pe, s["lx_done"], NT, b, NT * db + n - NT + 1)
                    jb_free()
                    for k in range(NF):
                        last = nc.tensor.transpose(jb[:, k * P:(k + 1) * P],
                                                   stage[slot_of(name)][:, k * P:(k + 1) * P], ident[:])
                    last.then_inc(s["t_mm"], 1)
                    jb_held(s["t_lo"], 8, b, 8 * db + n + 1)
                elif kind == "RT":
                    wait(pe, s["lr_done"], NT, b, -NT + n + 1)
                    jb_free()
                    for k in range(NF):
                        last = nc.tensor.transpose(jb[:, k * P:(k + 1) * P], x2[:, k * P:(k + 1) * P], ident[:])
                    last.then_inc(s["rt_mm"], 1)
                    jb_held(s["rt_done"], NT, b, -NT + n + 1)
                elif kind == "RL":
                    wait(pe, s["rt_done"], NT, b, -NT + n + 1)
                    jb_free()
                    for k in range(NF):
                        last = nc.tensor.matmul(jb[k * HD:(k + 1) * HD, 0:P], rw_pad[:, k, :], x2_t[:, k, :],
                                                start=True, stop=True)
                    last.then_inc(s["rl_mm"], 1)
                    jb_held(s["rl_done"], NT, b, -NT + n + 1)
                elif kind == "RS":
                    wait(pe, s["rl_done"], NT, b, -NT + n + 1)
                    jb_free()
                    nc.tensor.matmul(jb[:, 0:E], part[:], sel[:], start=True, stop=True).then_inc(s["rs_mm"], 1)
                    jb_held(s["rs_done"], NT, b, -NT + n + 1)
                elif kind == "RC":
                    wait(pe, s["oh_done"], NT, b, -NT + n + 1)
                    jb_free()
                    nc.tensor.matmul(jb[:, 0:E], before[:], chosen[:], start=True, stop=True)
                    nc.tensor.matmul(jb[:, E:2 * E], ones_b[:], chosen[:], start=True, stop=True).then_inc(s["rc_mm"], 1)
                    jb_held(s["rc_done"], NT, b, -NT + n + 1)

            def wait_staged_pe(name, b, db):
                n, k = load_count(name)
                wait(pe, staged[name], 16 * n, b, 16 * n * (db + 1) + 16 * (k + 1))

            for it in PROLOGUE:
                item(*split(it), 0, 0)
            item("Q", 0, 0, 0)
            item("K", 0, 0, 0)
            for k in range(8):
                item("M", k, -1, 0)
            item("MT", 0, -1, 0)
            item("Q", 0, 1, 0)
            item("K", 0, 1, 0)

            def body(b, first=False, last=False):
                jb_held(s["mt_copied"], 4, b, 1)
                if first:
                    jb_held(s["lo_done"], 8, 0, 4)
                for c, kind, n in steps(b, first, last):
                    if kind in ("Q", "K"):
                        db, tc = target(c)
                        item(kind, n, tc, b, db)
                    elif kind == "T":
                        item(kind, n, c, b, 1)
                    else:
                        item(kind, n, c, b)

            all_batches(nc.tensor, body)
            for it in EPILOGUE:
                item(*split(it), 0, B)

        @block.scalar
        def _(act):
            act.wait_ge(s["c_in0"], 16 * 5)
            nc.scalar.activation(tanh_g[:], g_all[:], ACT.Tanh).then_inc(s["a_const"], 1)
            for n in range(4 * NF):
                i, k = n // NF, n % NF
                act.wait_ge(s["w_mm"], n + 1)
                nc.scalar.activation(w_hi[i][:, k, :], sc[:, n % 4, :], ACT.Copy).then_inc(s["w_hi_done"], 1)

            def item(kind, n, c, b, db=0):
                u4 = 4 * db + c
                if kind == "A" and n < NT:
                    for h2 in range(2):
                        wait(act, s["st_done"], 32, b, 8 * u4 + 2 * n + h2 + 1)
                        wait(act, s["pv_done"], 16, b, 4 * u4 + n - 1)
                        wait(act, s["acc_done"], 24, b, 6 * u4 + (h2 + 1 if n >= 2 else 2 * n - 4 + h2 + 1))
                        nc.scalar.activation(probs[:, n % 2, 2 * h2:2 * h2 + 2, :], sc[:, 2 * h2:2 * h2 + 2, :],
                                             ACT.Exp, scale=SCALE).then_inc(s["exp_done"], 1)
                elif kind == "OU":
                    wait(act, s["pv_done"], 16, b, 4 * u4)
                    wait(act, s["nm_done"], 4, b, u4 - 1)
                    nc.scalar.activation(heads_raw[:], hb[:], ACT.Copy).then_inc(s["ou_done"], 1)
                elif kind in ("Q", "K"):
                    i = 0 if kind == "Q" else 1
                    wait(act, s["qk_mm"], 8, b, 2 * u4 + i + 1)
                    wait(act, s["stacked"], 4 * 16 * 24, b, 16 * 24 * u4)
                    nc.scalar.activation(qk_hi[:, i, :], jb[:], ACT.Identity,
                                         bias=bias[:, i, c:c + 1]).then_inc(s["hi_done"], 1)
                elif kind == "T":
                    wait(act, s["t_mm"], 8, b, 8 * db + n + 1)
                    dst = (c_hi if n < NT else xn_hi)[:, :, (n % NT) * P:(n % NT + 1) * P]
                    nc.scalar.activation(dst, jb[:, :].rearrange("p (k q) -> p k q", q=P), ACT.Copy)\
                        .then_inc(s["t_hi"], 1)
                elif kind == "V":
                    wait(act, s["v_mm"], NT, b, n + 1)
                    nc.scalar.activation(values[:, n, :], jb[:], ACT.Copy).then_inc(s["v_done"], 1)
                elif kind == "MT":
                    wait(act, s["mt_mm"], 4, b, u4 + 2)
                    wait(act, s["max_rows_in"], 128, b, 32 * (u4 + 1))
                    nc.scalar.activation(max_rows[:], jb[0:32, 0:P], ACT.Copy).then_inc(s["mt_copied"], 1)
                    wait(act, s["mt_copied"], 4, b, u4 + 2)
                    for j in range(2):
                        act.dma_start(q_stack[(c + 1) % 2][MAXROW + j:MAXROW + j + 1, :].bitcast(F32),
                                      max_rows[16 * j:16 * (j + 1), :].bitcast(F32)).then_inc(s["max_rows_in"], 16)
                elif kind == "RT":
                    wait(act, s["rt_mm"], NT, b, -NT + n + 1)
                    nc.scalar.activation(x2_t[:, :, :], jb[:, :].rearrange("p (k q) -> p k q", q=P), ACT.Copy)\
                        .then_inc(s["rt_done"], 1)
                elif kind == "RL":
                    wait(act, s["rl_mm"], NT, b, -NT + n + 1)
                    nc.scalar.activation(part[:], jb[:, 0:P], ACT.Copy).then_inc(s["rl_done"], 1)
                elif kind == "RS":
                    wait(act, s["rs_done"], NT, b, -NT + n + 1)
                    nc.scalar.activation(rt[:, 8:16], rt[:, 0:8], ACT.Exp, bias=rt[:, 17:18],
                                         accum_out=rt[:, 18:19]).then_inc(s["rs_exp"], 1)

            for it in PROLOGUE:
                item(*split(it), 0, 0)
            item("Q", 0, 0, 0)
            item("K", 0, 0, 0)
            item("MT", 0, -1, 0)
            item("Q", 0, 1, 0)
            item("K", 0, 1, 0)

            def body(b, first=False, last=False):
                for c, kind, n in steps(b, first, last):
                    if kind in ("Q", "K"):
                        db, tc = target(c)
                        item(kind, n, tc, b, db)
                    elif kind == "T":
                        item(kind, n, c, b, 1)
                    else:
                        item(kind, n, c, b)

            all_batches(nc.scalar, body)
            for it in EPILOGUE:
                item(*split(it), 0, B)

        @block.vector
        def _(dve):
            def chain(sem_, per, b, offset):
                k = [0]

                def link(ins, alone=None):
                    k[0] += 1
                    assert k[0] <= per[1]
                    ins.then_inc(sem_, 1)
                    wait(dve, sem_, per[0] * per[1], b, offset * per[1] + k[0], alone)
                return link

            dve.sem_inc(s["began"], 1)
            nc.vector.memset(rw_pad[:], 0.0).then_inc(s["d_const"], 1)
            nc.vector.memset(ones[:], 1.0).then_inc(s["d_const"], 1)
            nc.vector.memset(ones_b[:], 1.0).then_inc(s["d_const"], 1)
            for i in range(2):
                nc.vector.memset(k_stack[i][MAXROW:P, :].bitcast(F32), -1.0).then_inc(s["d_const"], 1)
            dve.wait_ge(s["a_const"], 1)
            dve.wait_ge(s["row_out0"], 16)
            dve.wait_ge(s["row_out1"], 16)
            dve.wait_ge(s["listed0"], 16)
            dve.wait_ge(s["listed1"], 16)
            nc.vector.tensor_scalar(gbo[:], gbo[:], tanh_g[:, 0:1], None, ALU.mult).then_inc(s["p_init"], 1)
            for n in range(4 * NF):
                i, k = n // NF, n % NF
                dve.wait_ge(s["w_hi_done"], n + 1)
                nc.vector.tensor_tensor(w_lo[i][:, k, :], sc[:, n % 4, :], w_hi[i][:, k, :].bitcast(F32),
                                        ALU.subtract).then_inc(s["w_lo_done"], 1)
            dve.wait_ge(s["p_const"], 5)

            def layernorm_stats(link, src, st):
                nc.vector.bn_stats(st[:, 0:6], src)
                nc.vector.drain()
                link(nc.vector.bn_aggr(st[:, 6:8], st[:, 0:6]))
                return nc.vector.tensor_scalar(st[:, 8:9], st[:, 7:8], EPS, None, ALU.add)

            def item(kind, n, c, b, db=0):
                u4 = 4 * db + c
                if kind == "M":
                    wait(dve, s["ms_done"], 32, b, 8 * (u4 + 1) + n + 1)
                    if n == 0:
                        wait(dve, s["mc_chain"], 4, b, u4 + 1)
                    nc.vector.tensor_reduce(maxima[:, 2 * n:2 * n + 2], mb[:, :, :], AX.X, ALU.max)\
                        .then_inc(s["mx_done"], 1)
                    if n == 7:
                        wait(dve, s["mx_done"], 32, b, 8 * (u4 + 2))
                        wait(dve, s["mt_mm"], 4, b, u4 + 1)
                        nc.vector.tensor_copy(max_parts[:, 0:16], maxima[:]).then_inc(s["mc_chain"], 1)
                        wait(dve, s["mc_chain"], 4, b, u4 + 2)
                        nc.vector.tensor_tensor(max_parts[:, 16:32], maxima[:], max_parts[:, 0:16].bitcast(F32),
                                                ALU.subtract).then_inc(s["mc_done"], 1)
                elif kind == "SUM":
                    wait(dve, s["sum_mm"], 4, b, u4)
                    nc.vector.reciprocal(recip[:], jb[:]).then_inc(s["sum_used"], 1)
                elif kind in ("NM", "NMP"):
                    if kind == "NM" and c == 1:
                        return
                    g = u4 - 1 if kind == "NM" else u4 - 2
                    gc, link = g % 4, chain(s["nm_chain"], (4, 2), b, g)
                    wait(dve, s["ou_done"], 4, b, g + 1)
                    wait(dve, s["sum_used"], 4, b, g + 1)
                    if gc == 0:
                        wait(dve, s["op_mm"], NT, b, NT * (g // 4))
                    link(nc.vector.tensor_tensor(heads_raw[:], heads_raw[:], recip[:], ALU.mult))
                    link(nc.vector.tensor_scalar(heads_hi[:, gc, :], heads_raw[:], bias[:, 2, gc:gc + 1], None, ALU.add))
                    nc.vector.scalar_tensor_tensor(heads_lo[:, gc, :], heads_raw[:], bias[:, 2, gc:gc + 1],
                                                   heads_hi[:, gc, :].bitcast(F32), ALU.add, ALU.subtract)\
                        .then_inc(s["nm_done"], 1)
                elif kind in ("Q", "K"):
                    i = 0 if kind == "Q" else 1
                    wait(dve, s["hi_done"], 8, b, 2 * u4 + i + 1)
                    nc.vector.scalar_tensor_tensor(qk_lo[:, i, :], jb[:], bias[:, i, c:c + 1],
                                                   qk_hi[:, i, :].bitcast(F32), ALU.add, ALU.subtract)\
                        .then_inc(s["lo_done"], 1)
                elif kind == "LX":
                    name, link = f"X{n}", chain(s["lx_chain"], (NT, 1), b, NT * db + n)
                    m, k = load_count(name)
                    wait(dve, staged[name], 16 * m, b, 16 * m * db + 16 * (k + 1))
                    layernorm_stats(link, stage[slot_of(name)][:], st1[n % 2]).then_inc(s["lx_var"], 1)
                elif kind == "T":
                    hi, lo = (c_hi, c_lo) if n < NT else (xn_hi, xn_lo)
                    wait(dve, s["t_hi"], 8, b, 8 * db + n + 1)
                    cols = slice((n % NT) * P, (n % NT + 1) * P)
                    nc.vector.tensor_tensor(lo[:, :, cols], jb[:, :].rearrange("p (k q) -> p k q", q=P),
                                            hi[:, :, cols].bitcast(F32), ALU.subtract).then_inc(s["t_lo"], 1)
                elif kind == "XA":
                    st, name = st1[n % 2], f"X{n}"
                    wait(dve, s["lx_pow"], NT, b, NT * db + n + 1)
                    nc.vector.tensor_scalar(stage[slot_of(name)][:], stage[slot_of(name)][:], st[:, 6:7], st[:, 9:10],
                                            ALU.subtract, ALU.mult).then_inc(s["lx_done"], 1)
                elif kind == "OP":
                    name = f"R{n}"
                    wait(dve, s["op_mm"], NT, b, -NT + n + 1)
                    wait(dve, s["xb_done"], NT, b, -NT + n + 1)
                    wait(dve, s[f"row_out{n % 2}"], 32, b, -32 + 16 * (n // 2) + 16)
                    nc.vector.scalar_tensor_tensor(row[n % 2][:, 0:D], jb[:], tanh_g[:, 0:1], stage[slot_of(name)][:],
                                                   ALU.mult, ALU.add).then_inc(s["x1_done"], 1)
                elif kind == "LR":
                    link = chain(s["lr_chain"], (NT, 4), b, n - NT)
                    wait(dve, s["x1_done"], NT, b, -NT + n + 1)
                    r = row[n % 2]
                    layernorm_stats(link, r[:, 0:D], st2[n % 2]).then_inc(s["lr_var"], 1)
                elif kind == "RT":
                    link = chain_from(s["lr_chain"], (NT, 4), b, n - NT, 1)
                    r, st = row[n % 2], st2[n % 2]
                    wait(dve, s["lr_pow"], NT, b, -NT + n + 1)
                    link(nc.vector.tensor_scalar(st[:, 10:11], st[:, 6:7], st[:, 9:10], -1.0, ALU.mult, ALU.mult))
                    link(nc.vector.tensor_copy(r[:, D:D + 1], st[:, 9:10]))
                    link(nc.vector.tensor_copy(r[:, D + 1:D + 2], st[:, 10:11]))
                    nc.vector.tensor_scalar(x2[:], r[:, 0:D], st[:, 9:10], st[:, 10:11], ALU.mult, ALU.add)\
                        .then_inc(s["lr_done"], 1)
                elif kind == "RS":
                    link = chain(s["rs_chain"], (NT, 8), b, n - NT)
                    wait(dve, s["rs_mm"], NT, b, -NT + n + 1)
                    link(nc.vector.tensor_tensor(rt[:, 0:8], jb[:, 0:E], rb_all[:], ALU.add))
                    link(nc.vector.tensor_reduce(rt[:, 16:17], rt[:, 0:8], AX.X, ALU.max))
                    nc.vector.tensor_scalar(rt[:, 17:18], rt[:, 16:17], -1.0, None, ALU.mult).then_inc(s["rs_done"], 1)
                    link(nc.vector.tensor_scalar(rt[:, 24:32], rt[:, 0:8], rt[:, 16:17], float(-E), ALU.is_equal, ALU.mult))
                    link(nc.vector.tensor_tensor(rt[:, 32:40], rt[:, 24:32], numbers[:], ALU.add))
                    link(nc.vector.tensor_reduce(rt[:, 20:21], rt[:, 32:40], AX.X, ALU.min))
                    link(nc.vector.tensor_scalar(rt[:, 40:48], rt[:, 32:40], rt[:, 20:21], None, ALU.is_equal))
                    nc.vector.tensor_copy(chosen[:], rt[:, 40:48]).then_inc(s["oh_done"], 1)
                    wait(dve, s["rs_exp"], NT, b, -NT + n + 1)
                    link(nc.vector.reciprocal(rt[:, 21:22], rt[:, 18:19]))
                    link(nc.vector.tensor_scalar(row[n % 2][:, D + 2:D + 3], rt[:, 21:22], tanh_g[:, 1:2], None, ALU.mult))
                elif kind == "RC":
                    link = chain(s["rc_chain"], (NT, 6), b, n - NT)
                    wait(dve, s["rc_mm"], NT, b, -NT + n + 1)
                    link(nc.vector.tensor_tensor(rt[:, 48:56], jb[:, 0:E], counts[:], ALU.add))
                    link(nc.vector.tensor_tensor(rt[:, 56:64], rt[:, 48:56], rt[:, 40:48], ALU.mult))
                    link(nc.vector.tensor_tensor(counts[:], jb[:, E:2 * E], counts[:], ALU.add))
                    link(nc.vector.reduce_sum(rt[:, 64:65], rt[:, 56:64], axis=AX.X))
                    wait(dve, s[f"listed{n % 2}"], 32, b, -32 + 16 * (n // 2) + 16)
                    link(nc.vector.tensor_copy(token_of[n % 2][:], token[:]))
                    link(nc.vector.tensor_scalar(token[:], token[:], float(P), None, ALU.add))
                    nc.vector.tensor_copy(dest[n % 2][:], rt[:, 64:65]).then_inc(s["rc_done"], 1)

            def chain_from(sem_, per, b, offset, at):
                link, k = None, [at]

                def linked(ins):
                    k[0] += 1
                    assert k[0] <= per[1]
                    ins.then_inc(sem_, 1)
                    wait(dve, sem_, per[0] * per[1], b, offset * per[1] + k[0])
                return linked

            def one(kind, n, c, b, db=0):
                if kind == "T" and n >= NT:
                    item("XA", n - NT, c, b, db)
                item(kind, n, c, b, db)

            for it in PROLOGUE:
                one(*split(it), 0, 0)
            item("Q", 0, 0, 0)
            item("K", 0, 0, 0)
            for k in range(8):
                item("M", k, -1, 0)
            item("Q", 0, 1, 0)
            item("K", 0, 1, 0)

            def body(b, first=False, last=False):
                for c, kind, n in steps(b, first, last):
                    if kind in ("Q", "K"):
                        db, tc = target(c)
                        item(kind, n, tc, b, db)
                    elif kind in ("T", "LX"):
                        one(kind, n, c, b, 1)
                    else:
                        item(kind, n, c, b)

            all_batches(nc.vector, body)
            for it in EPILOGUE:
                item(*split(it), 0, B)

        @block.gpsimd
        def _(pool):
            empty = x2[:, 0:E * TOKENS // P]
            nc.gpsimd.memset(empty, float(TOKENS)).then_inc(s["empty"], 1)
            pool.wait_ge(s["empty"], 1)
            halves = lists_dram.rearrange("(h p f) a -> h p (f a)", h=2, p=P)
            for j in range(2):
                pool.dma_start(halves[j], empty[:, 0:E * TOKENS // P // 2]).then_inc(s[f"listed{j}"], 16)
            nc.gpsimd.memset(ident[:], 0.0).then_inc(s["p_const"], 1)
            pool.wait_ge(s["p_const"], 1)
            nc.gpsimd.affine_select(out=ident[:], in_=ident[:], compare_op=ALU.not_equal, fill=1.0, base=0,
                                    pattern=[[-1, P]], channel_multiplier=1).then_inc(s["p_const"], 1)
            nc.gpsimd.iota(numbers[:], [[1, E]], base=0, channel_multiplier=0,
                           allow_small_or_imprecise_dtypes=True).then_inc(s["p_const"], 1)
            nc.gpsimd.iota(token[:], [[0, 1]], base=0, channel_multiplier=1,
                           allow_small_or_imprecise_dtypes=True).then_inc(s["p_const"], 1)
            nc.gpsimd.iota(counts[:], [[TOKENS, E]], base=0, channel_multiplier=0,
                           allow_small_or_imprecise_dtypes=True).then_inc(s["p_const"], 1)
            nc.gpsimd.memset(minus_half[:], -0.5).then_inc(s["p_const"], 1)
            nc.gpsimd.memset(sel[:], 0.0).then_inc(s["p_const"], 1)
            pool.wait_ge(s["p_const"], 7)
            for k in range(NF):
                nc.gpsimd.affine_select(out=sel[:], in_=sel[:], compare_op=ALU.not_equal, fill=1.0, base=-k * HD,
                                        pattern=[[-1, E]], channel_multiplier=1).then_inc(s["p_const"], 1)
                pool.wait_ge(s["p_const"], 8 + k)
            nc.gpsimd.memset(before[:], 1.0).then_inc(s["p_const"], 1)
            pool.wait_ge(s["p_const"], 12)
            nc.gpsimd.affine_select(out=before[:], in_=before[:], compare_op=ALU.is_gt, fill=0.0, base=0,
                                    pattern=[[1, P]], channel_multiplier=-1).then_inc(s["p_init"], 1)

            def item(kind, n, c, b, db=0):
                u4 = 4 * db + c
                if kind == "A" and 1 <= n < NT:
                    for h2 in range(2):
                        two = slice(2 * h2, 2 * h2 + 2)
                        wait(pool, s["exp_done"], 32, b, 8 * u4 + 2 * n + h2 + 1, s["began"])
                        if n == 1:
                            wait(pool, s["sum_mm"], 4, b, u4, s["began"])
                            in0 = probs[:, 0, two, :]
                        else:
                            wait(pool, s["acc_done"], 24, b, 6 * u4 + 2 * (n - 2) + h2 + 1, s["began"])
                            in0 = psum_keys[:, two, :]
                        nc.gpsimd.tensor_tensor(psum_keys[:, two, :], in0, probs[:, n % 2, two, :], ALU.add)\
                            .then_inc(s["acc_done"], 1)
                elif kind == "LX":
                    wait(pool, s["lx_var"], NT, b, NT * db + n + 1, s["began"])
                    st = st1[n % 2]
                    nc.gpsimd.tensor_tensor(st[:, 9:10], st[:, 8:9], minus_half[:], ALU.pow).then_inc(s["lx_pow"], 1)
                elif kind == "LR":
                    wait(pool, s["lr_var"], NT, b, -NT + n + 1, s["began"])
                    st = st2[n % 2]
                    nc.gpsimd.tensor_tensor(st[:, 9:10], st[:, 8:9], minus_half[:], ALU.pow).then_inc(s["lr_pow"], 1)
                elif kind == "OP":
                    name = f"R{n}"
                    m, k = load_count(name)
                    wait(pool, staged[name], 16 * m, b, -16 * m + 16 * (k + 1), s["began"])
                    tile = stage[slot_of(name)]
                    nc.gpsimd.tensor_tensor(tile[:], tile[:], gbo[:], ALU.add).then_inc(s["xb_done"], 1)
                elif kind == "RC":
                    wait(pool, s["rc_done"], NT, b, -NT + n + 1, s["began"])
                    nc.gpsimd.indirect_dma_start(
                        out=lists_dram[:, :], out_offset=bass.IndirectOffsetOnAxis(ap=dest[n % 2][:, 0:1].bitcast(U32), axis=0),
                        in_=token_of[n % 2][:, :], in_offset=None).then_inc(s[f"listed{n % 2}"], 16)

            pool.wait_ge(s["p_const"], 12)
            for it in PROLOGUE:
                item(*split(it), 0, 0)

            pool.wait_ge(s["p_init"], 2)

            def body(b, first=False, last=False):
                for c, kind, n in steps(b, first, last):
                    if kind == "LX":
                        item(kind, n, c, b, 1)
                    else:
                        item(kind, n, c, b)

            all_batches(nc.gpsimd, body)
            for it in EPILOGUE:
                item(*split(it), 0, B)
            for j in range(2):
                pool.wait_ge(s[f"listed{j}"], 16 + 32 * B)


def expert_part(nc, ew, eb, rows_dram, lists_dram, counts, ident, out_rows):
    with ExitStack() as es:
        def sb(name, shape, dt=F32):
            return es.enter_context(nc.sbuf_tensor(name, shape, dt))

        def ps(name, shape):
            return es.enter_context(nc.psum_tensor(name, shape, F32))

        def sem(name):
            return es.enter_context(nc.semaphore("e_" + name))

        e_hi = sb("e_hi", [P, E, NF, D], F32R)
        e_lo = sb("e_lo", [P, E, NF, D], F32R)
        raw = [sb(f"raw{i}", [P, NF, D]) for i in range(2)]
        eb_all = sb("eb_all", [P, E, D])
        got = [sb(f"got{i}", [P, ROW]) for i in range(2)]
        xt_hi = [sb(f"xt_hi{i}", [P, NF, P], F32R) for i in range(2)]
        xt_lo = [sb(f"xt_lo{i}", [P, NF, P], F32R) for i in range(2)]
        xe = [sb(f"xe{i}", [P, D]) for i in range(2)]
        done = [sb(f"done{i}", [P, D]) for i in range(2)]
        small = sb("small", [P, 6, E])
        plan = sb("plan", [P, 8])
        one = sb("one", [P, E])
        tiles_i = sb("tiles_i", [P, E], I32)
        number = sb("number", [P, E])
        lane = sb("lane", [P, 1])
        list_row = sb("list_row", [P, 1], I32)
        tokens = sb("tokens", [P, P])
        expert_i = sb("expert_i", [1, P], I32)
        src_i = sb("src_i", [P, TILES], I32)
        dst_i = sb("dst_i", [P, TILES], I32)
        index = [sb(f"index{i}", [P, 1], I32) for i in range(2)]
        target = [sb(f"target{i}", [P, 1], I32) for i in range(2)]
        tp = [ps(f"tp{i}", [P, NF * P]) for i in range(2)]
        yb = [ps(f"yb{i}", [P, D]) for i in range(2)]

        s = {n: sem(n) for n in ("w_in0", "w_in1", "w_hi", "w_lo", "eb_in", "const", "chain", "src_ready", "plan_ready",
                                 "in0", "in1", "xe", "tp", "hi", "lo", "y", "row_ready", "tokens_in", "tokens_ok", "plan_mm", "y1", "fin", "out0", "out1")}
        block = es.enter_context(nc.Block())
        LAST = TILES - 1

        def at(eng, sem_, pair, j, off, per=1, alone=False):
            if isinstance(pair, int):
                v = per * (2 * pair + j) + off
                if v > 0:
                    eng.wait_ge(sem_, v)
            else:
                assert per * (2 + j) + off > 0
                value = pair * (2 * per) + per * j + off
                if alone:
                    value = eng.snap(value)
                    eng.wait_ge(s["const"], 1)
                eng.wait_ge(sem_, value)

        def run(engine, body):
            for j in range(2):
                body(0, j)
            with engine.Fori(1, TILES // 2) as pair:
                for j in range(2):
                    body(pair, j)

        @block.sync
        def _(sp):
            sp.dma_start(eb_all[:, :, :], eb.partition_broadcast(P)).then_inc(s["eb_in"], 16)
            for e in range(E):
                if e >= 2:
                    sp.wait_ge(s["w_lo"], e - 1)
                sp.dma_start(raw[e % 2][:, :, :], ew[e].rearrange("(c p) d -> p c d", p=P)).then_inc(s[f"w_in{e % 2}"], 16)

        @block.scalar
        def _(act):
            for e in range(E):
                act.wait_ge(s[f"w_in{e % 2}"], 16 * (e // 2 + 1))
                nc.scalar.activation(e_hi[:, e, :, :], raw[e % 2][:, :, :], ACT.Copy).then_inc(s["w_hi"], 1)

            def body(pair, j):
                g = got[j]
                at(act, s[f"in{j}"], pair, j, 16 - 8 * j, 8)
                at(act, s["tp"], pair, j, -1)
                nc.scalar.activation(xe[j][:], g[:, 0:D], ACT.Identity, scale=g[:, D:D + 1], bias=g[:, D + 1:D + 2])\
                    .then_inc(s["xe"], 1)
                at(act, s["tp"], pair, j, 1)
                at(act, s["y"], pair, j, -1)
                nc.scalar.activation(xt_hi[j][:, :, :], tp[j][:, :].rearrange("p (k q) -> p k q", q=P), ACT.Copy)\
                    .then_inc(s["hi"], 1)
            run(nc.scalar, body)

        @block.vector
        def _(dve):
            k = [0]

            def link(ins):
                k[0] += 1
                ins.then_inc(s["chain"], 1)
                dve.wait_ge(s["chain"], k[0])

            dve.wait_ge(s["const"], 2)
            cnt, ntl, end, tmp, past, past_tiles = (small[:, i, :] for i in range(6))
            link(nc.vector.memset(one[:], 1.0))
            link(nc.vector.scalar_tensor_tensor(cnt, number[:], float(-TOKENS), counts[:], ALU.mult, ALU.add))
            link(nc.vector.tensor_scalar(tmp, cnt, 1.0 / P, (P - 1.0) / P - (P - 1.0) / (2 * P), ALU.mult, ALU.add))
            link(nc.vector.tensor_copy(tiles_i[:], tmp))
            link(nc.vector.tensor_copy(ntl, tiles_i[:]))
            link(nc.vector.tensor_tensor_scan(end, one[:], ntl, 0.0, ALU.mult, ALU.add))
            tile, expert, start, bad, in_list, t1 = (plan[:, i:i + 1] for i in range(6))
            link(nc.vector.tensor_scalar(t1, lane[:], 1.0, end[:, E - 1:E], ALU.add, ALU.min))
            link(nc.vector.tensor_scalar(tile, t1, 1.0, None, ALU.subtract))
            link(nc.vector.tensor_scalar(past, end, tile, None, ALU.is_le))
            link(nc.vector.reduce_sum(expert, past, axis=AX.X))
            link(nc.vector.tensor_tensor(past_tiles, past, ntl, ALU.mult))
            link(nc.vector.reduce_sum(start, past_tiles, axis=AX.X))
            link(nc.vector.tensor_tensor(in_list, tile, start, ALU.subtract))
            link(nc.vector.scalar_tensor_tensor(in_list, expert, float(TOKENS // P), in_list, ALU.mult, ALU.add))
            nc.vector.tensor_copy(list_row[:], in_list).then_inc(s["row_ready"], 1)
            link(nc.vector.tensor_tensor(bad, lane[:], tile, ALU.is_gt))
            link(nc.vector.tensor_scalar(bad, bad, float(2 * TOKENS), None, ALU.mult))
            dve.wait_ge(s["tokens_in"], 16)
            nc.vector.tensor_scalar(tokens[:], tokens[:], bad, None, ALU.add).then_inc(s["tokens_ok"], 1)
            dve.wait_ge(s["plan_mm"], 1)
            nc.vector.tensor_scalar(src_i[:], tp[0][:, 0:TILES], float(TOKENS - 1), None, ALU.min).then_inc(s["src_ready"], 1)
            nc.vector.tensor_copy(dst_i[:], tp[0][:, 0:TILES]).then_inc(s["plan_ready"], 1)
            nc.vector.tensor_copy(expert_i[:], tp[1][0:1, 0:P]).then_inc(s["plan_ready"], 1)
            for e in range(E):
                dve.wait_ge(s["w_hi"], e + 1)
                nc.vector.tensor_tensor(e_lo[:, e, :, :], raw[e % 2][:, :, :], e_hi[:, e, :, :].bitcast(F32),
                                        ALU.subtract).then_inc(s["w_lo"], 1)
            dve.wait_ge(s["eb_in"], 16)
            dve.wait_ge(s["plan_ready"], 2)

            def body(pair, j):
                at(dve, s["hi"], pair, j, 1)
                nc.vector.tensor_tensor(xt_lo[j][:, :, :], tp[j][:, :].rearrange("p (k q) -> p k q", q=P),
                                        xt_hi[j][:, :, :].bitcast(F32), ALU.subtract).then_inc(s["lo"], 1)
                t = 2 * pair + j
                e = nc.vector.value_load(expert_i[0:1, bass.ds(t, 1)], min_val=0, max_val=E - 1)
                g = got[j]
                at(dve, s[f"out{j}"], pair, j, -8 * j, 8)
                at(dve, s["y"], pair, j, 1)
                nc.vector.tensor_tensor(done[j][:], yb[j][:], eb_all[:, bass.ds(e, 1), :].rearrange("p a d -> p (a d)"),
                                        ALU.add).then_inc(s["y1"], 1)
                at(dve, s["y1"], pair, j, 1)
                nc.vector.scalar_tensor_tensor(done[j][:], done[j][:], g[:, D + 2:D + 3], g[:, 0:D], ALU.mult, ALU.add)\
                    .then_inc(s["fin"], 1)
            run(nc.vector, body)

        @block.tensor
        def _(pe):
            pe.wait_ge(s["tokens_ok"], 1)
            nc.tensor.transpose(tp[0][:, 0:P], tokens[:], ident[:])
            nc.tensor.transpose(tp[1][0:1, 0:P], plan[:, 1:2], ident[:]).then_inc(s["plan_mm"], 1)
            pe.wait_ge(s["plan_ready"], 2)
            pe.wait_ge(s["w_lo"], E)

            def body(pair, j):
                at(pe, s["xe"], pair, j, 1)
                at(pe, s["lo"], pair, j, -1)
                for i in range(NF):
                    last = nc.tensor.transpose(tp[j][:, i * P:(i + 1) * P], xe[j][:, i * P:(i + 1) * P], ident[:])
                last.then_inc(s["tp"], 1)
                e = nc.tensor.value_load(expert_i[0:1, bass.ds(2 * pair + j, 1)], min_val=0, max_val=E - 1)
                at(pe, s["lo"], pair, j, 1)
                at(pe, s["y1"], pair, j, -1)
                for i in range(NF):
                    for n, (a, w) in enumerate(((xt_hi, e_hi), (xt_lo, e_hi), (xt_hi, e_lo))):
                        last = nc.tensor.matmul(yb[j][:], a[j][:, i, :],
                                                w[:, bass.ds(e, 1), i, :].rearrange("p a d -> p (a d)"),
                                                start=(i == 0 and n == 0), stop=(i == NF - 1 and n == 2))
                last.then_inc(s["y"], 1)
            run(nc.tensor, body)

        @block.gpsimd
        def _(pool):
            nc.gpsimd.iota(number[:], [[1, E]], base=0, channel_multiplier=0,
                           allow_small_or_imprecise_dtypes=True).then_inc(s["const"], 1)
            nc.gpsimd.iota(lane[:], [[0, 1]], base=0, channel_multiplier=1,
                           allow_small_or_imprecise_dtypes=True).then_inc(s["const"], 1)
            pool.wait_ge(s["row_ready"], 1)
            lists = lists_dram.rearrange("(r q) a -> r (q a)", q=P)
            nc.gpsimd.indirect_dma_start(
                out=tokens[:, :], out_offset=None, in_=lists,
                in_offset=bass.IndirectOffsetOnAxis(ap=list_row[:, 0:1].bitcast(U32), axis=0)).then_inc(s["tokens_in"], 16)
            pool.wait_ge(s["src_ready"], 1)
            pool.wait_ge(s["plan_ready"], 2)

            def gather(pair, t, j):
                nc.gpsimd.tensor_copy(index[j][:], src_i[:, bass.ds(t, 1)])
                nc.gpsimd.drain()
                nc.gpsimd.indirect_dma_start(
                    out=got[j][:, :], out_offset=None, in_=rows_dram[:, :],
                    in_offset=bass.IndirectOffsetOnAxis(ap=index[j][:, 0:1].bitcast(U32), axis=0)).then_inc(s[f"in{j}"], 16)

            def body(pair, j):
                t = 2 * pair + j
                at(pool, s["fin"], pair, j, -1, alone=True)
                gather(pair, t, j)
                if not isinstance(pair, int) or j == 1:
                    at(pool, s["fin"], pair, j, 0, alone=True)
                    send(pair, j)

            def send(pair, j):
                t, slot = 2 * pair + j - 1, (j + 1) % 2
                nc.gpsimd.tensor_copy(target[slot][:], dst_i[:, bass.ds(t, 1)])
                nc.gpsimd.drain()
                nc.gpsimd.indirect_dma_start(
                    out=out_rows[:, :],
                    out_offset=bass.IndirectOffsetOnAxis(ap=target[slot][:, 0:1].bitcast(U32), axis=0),
                    in_=done[slot][:, :], in_offset=None, bounds_check=TOKENS - 1, oob_is_err=False)\
                    .then_inc(s[f"out{slot}"], 16)
            run(nc.gpsimd, body)
            pool.wait_ge(s["fin"], TILES)
            send(TILES // 2, 0)
            pool.wait_ge(s["out0"], 8 * TILES)
            pool.wait_ge(s["out1"], 8 * TILES)


_INS = ["x", "ctx_1024", "g_xattn", "g_ffn", "L0_xattn_Wq", "L0_xattn_bq", "L0_xattn_Wk", "L0_xattn_bk",
        "L0_xattn_Wv", "L0_xattn_bv", "L0_xattn_Wo", "L0_xattn_bo", "L0_ffn_router_w", "L0_ffn_router_b",
        "L0_ffn_expert_w", "L0_ffn_expert_b"]


def kernel(**inputs):
    import numpy as np
    import concourse.bacc as bacc
    from concourse.bass_utils import run_bass_kernel_spmd

    nc = bacc.Bacc("TRN2", target_bir_lowering=False, num_devices=1)
    arrays, args = {}, []
    for name in _INS:
        a = np.ascontiguousarray(inputs[name])
        arrays[f"in_{name}"] = a
        args.append(nc.dram_tensor(f"in_{name}", a.shape, mybir.dt.from_np(a.dtype), kind="ExternalInput").ap())
    out = nc.dram_tensor("out_x", [B, S, D], F32, kind="ExternalOutput").ap()
    build(nc, *args, out)
    r = run_bass_kernel_spmd(nc, [arrays], core_ids=[0])
    return r.results[0]["out_x"]
```

```python
from contextlib import ExitStack

import concourse.bass as bass
from concourse import mybir

F32 = mybir.dt.float32
F32R = mybir.dt.float32r
BF16 = mybir.dt.bfloat16
I32 = mybir.dt.int32
U32 = mybir.dt.uint32
ALU = mybir.AluOpType
ACT = mybir.ActivationFunctionType
AX = mybir.AxisListType

B, S, D = 8, 512, 512
HEADS, HD = 16, 32
E = 8
P = 128
NT = S // P
NF = D // P
HG = P // HD
TOKENS = B * S
SCALE = 1.0 / float(HD) ** 0.5
EPS = 1e-5
ROW = D + 3
MAXROW = 3 * HD
TILES = 40

ORDER = {
    "SP": [
        "ST RC0 OP0 OP1 RC1 T0 T1 T2 T3",
        "ST OP2 OP3 RC2 T4 T5",
        "ST",
        "ST T6 RC3 T7",
    ],
    "PE": [
        "V0 V1 SUM V2 M0 A0 SC M1 M2 M3 A1 M4 M5 M6 A2 Q NM K M7 M8 A3 M9 M10 M11 OP0 M12 OP1 V3 M13 M14 RT0 M15 RL0 RS0 A4 RC0 MT",
        "SUM M0 RT1 M1 SC M2 RL1 M3 M4 M5 M6 A0 Q A1 RS1 K T0 M7 A2 M8 T1 T2 T3 RC1 A3 M9 M10 M11 M12 M13 A4 M14 M15 OP2 MT",
        "M0 M1 NMP OP3 M2 SUM M3 SC RT2 RL2 M4 M5 M6 A0 RS2 M7 M8 A1 M9 M10 T4 M11 M12 A2 M13 M14 T5 A3 T6 T7 NM M15 Q K A4 RC2 MT RT3",
        "A0 SUM A1 M0 M1 M2 M3 A2 M4 M5 M6 M7 Q M8 K A3 M9 M10 M11 SC M12 M13 M14 M15 NM RL3 RS3 A4 RC3 MT",
    ],
    "ACT": [
        "V0 OU V1 SUM V2 A0 A1 SC A2 Q NM K A3 NR0 V3 A4 RT0 RL0 RS0 NR1 MT",
        "SUM RT1 OU RL1 A0 A1 RS1 SC Q K T0 A2 T1 T2 T3 A3 A4 MT",
        "NMP SUM NR2 RT2 SC RL2 OU A0 A1 RS2 NR3 NX0 T4 NX1 A2 T5 NX2 NX3 T6 T7 A3 Q A4 K MT RT3 NM",
        "OU A0 A1 SUM A2 Q K SC A3 RL3 RS3 NM MT A4",
    ],
    "DVE": [
        "M0 SC M1 M2 M3 M4 M5 M6 NM Q NL M7 K M8 M9 M10 M11 OP0 LR0 M12 OP1 LR1 RT0 M13 M14 M15 MC RS0 RC0",
        "M0 M1 SC M2 M3 RG0 RT1 M4 M5 M6 RS1 RG1 Q K T0 M7 M8 T1 RC1 T2 T3 M9 M10 M11 M12 M13 M14 M15 MC OP2",
        "M0 LR2 LX0 M1 NMP OP3 M2 LR3 M3 SC NLP M4 M5 M6 RT2 RS2 LX1 M7 M8 RG2 M9 M10 LX2 T4 M11 M12 LX3 M13 M14 T5 T6 T7 M15 MC NM Q K RC2 RT3 NL",
        "M0 M1 M2 M3 M4 M5 M6 M7 M8 Q K M9 M10 SC M11 M12 M13 M14 M15 MC NM RS3 RG3 NL RC3",
    ],
    "POOL": [
        "A0 A1 OP0 A2 A3 OP1 A4",
        "A0 LR0 LR1 RC0 A1 A2 OP2 OP3 A3 LX0 RC1 LR2 LR3 LX1 A4",
        "A0 A1 LX2 LX3 A2 A3 A4",
        "A0 A1 A2 A3 A4 RC2 RC3",
    ],
}
NJB = 3
THROUGH_JB = {"M", "V", "SUM", "SC", "NM", "NMP", "Q", "K", "OP", "T", "RT", "RL", "RS", "RC", "MT"}
LOADS = ["R0", "R1", "C0", "C2", "C1", "C3", "R2", "R3", "X0", "X1", "X2", "X3"]
CONSUMER = {"R": ("OP", 0), "C": ("T", 0), "X": ("T", NT)}
NSLOT = 3
SLOTS = 4


EVERY_STEP = {"M", "SUM", "SC", "NM", "Q", "K", "MT"}


def split(item):
    kind = item.rstrip("0123456789")
    return kind, int(item[len(kind):] or 0)


def bank_of_items():
    banks, turn = {}, 0
    for c, step in enumerate(ORDER["PE"]):
        for item in step.split():
            kind, n = split(item)
            if kind in THROUGH_JB:
                banks[kind, n, c if kind in EVERY_STEP else None] = turn % NJB
                turn += 1
    return banks


def with_banks(items):
    turn = 0
    for item in items:
        kind, n = split(item)
        yield kind, n, (turn % NJB if kind in THROUGH_JB else None)
        turn += kind in THROUGH_JB


def slot_of(name):
    return LOADS.index(name) % NSLOT


def load_count(name):
    same = [x for x in LOADS if x[0] == name[0] and slot_of(x) == slot_of(name)]
    return len(same), same.index(name)


def wait(eng, sem, per, b, offset, alone=None):
    if isinstance(b, int):
        if per * b + offset > 0:
            eng.wait_ge(sem, per * b + offset)
    else:
        assert per + offset > 0
        value = b * per + offset
        if alone is not None:
            value = eng.snap(value)
            eng.wait_ge(alone, 1)
        eng.wait_ge(sem, value)


def tenant_before(name, first, last):
    loads = [m for m in LOADS if not (first and m[0] == "R") and not (last and m[0] != "R")]
    if name not in loads:
        return None, False
    earlier = [m for m in loads[:loads.index(name)] if slot_of(m) == slot_of(name)]
    return (earlier[-1] if earlier else None), True


def build(nc, x, ctx, g_xattn, g_ffn, wq, bq, wk, bk, wv, bv, wo, bo, rw, rb, ew, eb, out):
    rows_dram = nc.dram_tensor("rows", [TOKENS, ROW], F32, kind="Internal").ap()
    lists_dram = nc.dram_tensor("lists", [E * TOKENS, 1], F32, kind="Internal").ap()
    out_rows = out.rearrange("b s d -> (b s) d")
    with ExitStack() as keep:
        def kept(name, shape, dt=F32):
            return keep.enter_context(nc.sbuf_tensor(name, shape, dt))

        counts = kept("counts", [P, E])
        ident = kept("ident", [P, P])
        kept_tiles = attention_part(nc, keep, x, ctx, g_xattn, g_ffn, wq, bq, wk, bk, wv, bv, wo, bo, rw, rb,
                       rows_dram, lists_dram, counts, ident, ew)
        expert_part(nc, kept_tiles, eb, rows_dram, lists_dram, counts, ident, out_rows)


def attention_part(nc, keep, x, ctx, g_xattn, g_ffn, wq, bq, wk, bk, wv, bv, wo, bo, rw, rb, rows_dram, lists_dram,
                   counts, ident, ew):
    with ExitStack() as es:
        attention_only = ExitStack()

        def kept(name, shape, dt=F32):
            return keep.enter_context(nc.sbuf_tensor(name, shape, dt))

        def sb(name, shape, dt=F32):
            return attention_only.enter_context(nc.sbuf_tensor(name, shape, dt))

        def ps(name, shape):
            return es.enter_context(nc.psum_tensor(name, shape, F32))

        def sem(name):
            return es.enter_context(nc.semaphore(name))

        wo_hi, wo_lo = kept("wo_hi", [P, NF, D], F32R), kept("wo_lo", [P, NF, D], F32R)
        heads_hi = kept("heads_hi", [P, NF, S], F32R)
        heads_lo = kept("heads_lo", [P, NF, S], F32R)
        stage = [kept(f"stage{i}", [P, D]) for i in range(NSLOT)]
        row = [kept(f"row{i}", [P, ROW]) for i in range(2)]
        x2 = kept("x2", [P, D])
        x2_t = kept("x2_t", [P, NF, P])
        gbo = kept("gbo", [P, D])
        part = kept("part", [P, P])
        rw_pad = kept("rw_pad", [P, NF, HD])
        sel = kept("sel", [P, E])
        before = kept("before", [P, P], BF16)
        ones_b = kept("ones_b", [P, P], BF16)
        chosen = kept("chosen", [P, E], BF16)
        bias = kept("bias", [P, 3, NF])
        rb_all = kept("rb_all", [P, E])
        tiny = kept("tiny", [P, 8])
        numbers = kept("numbers", [P, E])
        st2 = [kept(f"st2_{i}", [P, 12]) for i in range(2)]
        rt = kept("rt", [P, 72])
        dests = kept("dests", [P, 2], I32)
        w_hi = [sb(f"w{n}_hi", [P, NF, D], F32R) for n in "qkv"] + [wo_hi]
        w_lo = [sb(f"w{n}_lo", [P, NF, D], F32R) for n in "qkv"] + [wo_lo]
        c_hi = sb("c_hi", [P, NF, S], F32R)
        c_lo = sb("c_lo", [P, NF, S], F32R)
        xn_hi = sb("xn_hi", [P, NF, S], F32R)
        xn_lo = sb("xn_lo", [P, NF, S], F32R)
        q_stack = [sb(f"q_stack{i}", [P, HG * S], F32R) for i in range(2)]
        k_stack = [sb(f"k_stack{i}", [P, HG * S], F32R) for i in range(2)]
        qk_hi = sb("qk_hi", [P, 2, S], F32R)
        qk_lo = sb("qk_lo", [P, 2, S], F32R)
        values = sb("values", [P, NT, D])
        probs = sb("probs", [P, 2, HG, S])
        psum_keys = sb("psum_keys", [P, HG, S])
        heads_raw = sb("heads_raw", [P, S])
        sums = sb("sums", [P, S])
        recip = sb("recip", [P, NT, HG])
        ones = sb("ones", [P, HD])
        g_all, tanh_g, minus_half, token = tiny[:, 0:2], tiny[:, 2:4], tiny[:, 4:5], tiny[:, 5:6]
        token_of = [tiny[:, 6:7], tiny[:, 7:8]]
        maxima = sb("maxima", [P, 16])
        max_parts = sb("max_parts", [P, 32], F32R)
        max_rows = sb("max_rows", [32, P], F32R)
        st1 = [sb(f"st1_{i}", [P, 12]) for i in range(2)]
        dest = [dests[:, 0:1], dests[:, 1:2]]

        sc = ps("sc", [P, HG, S])
        hb = ps("hb", [P, S])
        jbs = [ps(f"jb{i}", [P, S]) for i in range(NJB)]

        s = {n: sem(n) for n in (
            "began", "w_in", "empty", "c_in0", "c_in1", "w_mm", "w_hi_done", "w_lo_done", "p_const", "d_const", "p_init", "a_const",
            "st_done", "exp_done", "acc_done", "pv_done", "ms_done", "mx_done", "mc_done", "mc_chain", "mt_mm",
            "mt_copied", "max_rows_in", "sum_mm", "sum_used", "sc_mm", "sc_used", "wide_done", "nm_mm", "nm_hi", "ou_done", "nm_chain", "nm_done",
            "qk_mm", "hi_done", "lo_done", "v_mm", "v_done", "op_mm", "xb_done", "x1_done",
            "t_mm", "t_hi", "t_lo", "lx_chain", "lx_var", "lx_rstd", "lr_rstd", "rt_stats", "ew_in0", "ew_in1", "ew_hi", "ew_lo", "lx_pow", "lx_done",
            "lr_chain", "lr_var", "lr_pow", "lr_done", "rt_mm", "rt_done", "rl_mm", "rl_done",
            "rs_mm", "rs_chain", "rg_chain", "rs_done", "rs_exp", "oh_done", "rc_mm", "rc_chain", "rc_done", "row_out0", "row_out1", "listed0", "listed1")}
        stacked = [sem(f"stacked{h}") for h in range(HG)]
        by_slot = {key: sem(f"staged_{key[0]}_{key[1]}") for key in sorted({(n[0], slot_of(n)) for n in LOADS})}
        staged = {n: by_slot[n[0], slot_of(n)] for n in LOADS}
        nat = [probs[:, 0], probs[:, 1], psum_keys[:, :, :], values[:, :, :]]

        def wait_staged(eng, name, b):
            n, k = load_count(name)
            wait(eng, staged[name], 16 * n, b, 16 * (k + 1))

        def late(kind, u4):
            return u4 - 1 if kind == "NM" else u4 - 2

        def target(c):
            return (0, c + 2) if c < 2 else (1, c - 2)

        def skipped(kind, c, first, last):
            if first and kind in ("OP", "LR", "NR", "RT", "RL", "RS", "RG", "RC"):
                return True
            if first and c == 0 and kind in ("OU", "SUM", "SC", "NM", "NL"):
                return True
            if last and (kind in ("T", "LX", "NX") or (kind in ("Q", "K") and c >= 2) or (kind == "ST" and c >= 2) or
                         (kind in ("M", "MC", "MT") and c == 3)):
                return True
            return False

        banks = bank_of_items()

        def steps(engine, first=False, last=False):
            for c, step in enumerate(ORDER[engine]):
                for kind, n in map(split, step.split()):
                    if not skipped(kind, c, first, last):
                        like = {"NL": "NM", "NLP": "NMP"}.get(kind, kind)
                        yield c, kind, n, banks.get((like, n, c if like in EVERY_STEP else None))

        def all_batches(eng, body):
            body(0, first=True)
            with eng.Fori(1, B - 1) as b:
                body(b)
            body(B - 1, last=True)

        OPENING = "T0 T1 T2 LX0 T3 LX1 NX0 T4 NX1 LX2 T5 NX2 LX3 T6 NX3 T7 Q K".split()
        OPENING_2 = ["MC", "MT", "Q", "K"]
        CLOSING = ["OU", "SUM", "SC", "NM", "NL"]
        EPILOGUE = ("OP0 LR0 OP1 NR0 RT0 LR1 RL0 W0 RS0 RG0 NR1 RT1 RC0 RL1 W1 RS1 RG1 OP2 RC1 LR2 "
                    "W2 OP3 NR2 RT2 LR3 RL2 W3 RS2 RG2 NR3 RT3 RC2 RL3 W4 RS3 RG3 W5 RC3 W6 W7").split()

        def sync_program(sp, attention):
            def load(name, b):
                kind, t = name[0], int(name[1])
                src, tb = {"R": (x, b - 1), "C": (ctx, b + 1), "X": (x, b + 1)}[kind]
                rows_of = src[tb, t * P:(t + 1) * P, :] if isinstance(tb, int) else \
                    src[bass.ds(tb, 1), t * P:(t + 1) * P, :].rearrange("a p d -> (a p) d")
                sp.dma_start(stage[slot_of(name)][:], rows_of).then_inc(staged[name], 16)

            def load_after(kind, n, b, first=False, last=False):
                for name in LOADS:
                    before, there = tenant_before(name, first, last)
                    if there and before and (CONSUMER[before[0]][0], CONSUMER[before[0]][1] + int(before[1])) == (kind, n):
                        if kind == "OP":
                            wait(sp, s["x1_done"], NT, b, -NT + n + 1, s["began"])
                        else:
                            wait(sp, s["t_mm"], 8, b, 8 + n + 1, s["began"])
                        load(name, b)

            def first_loads(b, first=False, last=False):
                wait(sp, s["t_mm"], 8, b, 8 if not isinstance(b, int) or b < B else 0, s["began"])
                for name in LOADS:
                    before, there = tenant_before(name, first, last)
                    if there and before is None:
                        load(name, b)

            def load_expert(e):
                if e >= 2:
                    sp.wait_ge(s["ew_lo"], e - 1)
                sp.dma_start(raw[e % 2][:, :, :], ew[e].rearrange("(c p) d -> p c d", p=P)).then_inc(s[f"ew_in{e % 2}"], 16)

            def row_to_dram(n, b):
                wait(sp, s["rg_chain"], NT * 2, b, 2 * (n - NT) + 2, s["began"])
                wait(sp, s["rt_stats"], NT, b, n - NT + 1, s["began"])
                tb = b - 1
                dst = rows_dram[(tb * NT + n) * P:(tb * NT + n + 1) * P, :] if isinstance(b, int) else \
                    rows_dram[bass.ds(tb * S + n * P, P), :]
                sp.dma_start(dst, row[n % 2][:, :]).then_inc(s[f"row_out{n % 2}"], 16)

            if not attention:
                first_loads(B, last=True)
                for e in range(2):
                    load_expert(e)
                for kind, n, _ in with_banks(EPILOGUE):
                    if kind == "OP":
                        load_after(kind, n, B, last=True)
                    elif kind == "RC":
                        row_to_dram(n, B)
                    elif kind == "W" and n + 2 < E:
                        load_expert(n + 2)
                for j in range(2):
                    sp.wait_ge(s[f"row_out{j}"], 16 + 32 * B)
                return

            def stack(c, b, db):
                wait(sp, s["lo_done"], 8, b, 8 * db + 2 * c + 2, s["began"])
                for h in range(HG):
                    wait(sp, s["st_done"], 32, b, 32 * db + 8 * (c - 1) - (1 if h < 2 else 0), s["began"])
                    cols, rows = slice(h * S, (h + 1) * S), slice(h * HD, (h + 1) * HD)
                    for i, stk, parts in ((0, q_stack, (qk_hi, qk_hi, qk_lo)), (1, k_stack, (qk_hi, qk_lo, qk_hi))):
                        for j, src in enumerate(parts):
                            sp.dma_start(stk[c % 2][j * HD:(j + 1) * HD, cols].bitcast(F32),
                                         src[rows, i, :].bitcast(F32)).then_inc(stacked[h], 16)

            for i, w in enumerate((wq, wk, wv, wo)):
                sp.dma_start(nat[i], w.rearrange("(c p) i -> p c i", p=P)).then_inc(s["w_in"], 16)
                sp.wait_ge(s["w_in"], 16 * (i + 1))
            sp.dma_start(rb_all[:], rb.partition_broadcast(P)).then_inc(s["row_out0"], 16)
            sp.dma_start(gbo[:], bo.partition_broadcast(P)).then_inc(s["row_out1"], 16)
            for i, v in enumerate((bq, bk, bv)):
                sp.dma_start(bias[:, i, :], v.rearrange("(c p) -> p c", p=P), allow_slow_non_contiguous=True).then_inc(s["c_in0"], 16)
            sp.dma_start(g_all[:, 0:1], g_xattn.partition_broadcast(P)).then_inc(s["c_in0"], 16)
            sp.dma_start(g_all[:, 1:2], g_ffn.partition_broadcast(P)).then_inc(s["c_in0"], 16)
            sp.wait_ge(s["d_const"], 1)
            sp.dma_start(rw_pad[:, :, 0:E], rw.rearrange("(c p) e -> p c e", p=P)).then_inc(s["c_in1"], 16)

            inputs = [name for name in LOADS if name[0] != "R"]
            for n, name in enumerate(inputs):
                earlier = [m for m in inputs[:n] if slot_of(m) == slot_of(name)]
                if earlier:
                    sp.wait_ge(s["t_mm"], (0 if earlier[-1][0] == "C" else NT) + int(earlier[-1][1]) + 1)
                load(name, -1)
            stack(0, 0, 0)
            stack(1, 0, 0)

            def body(b, first=False, last=False):
                first_loads(b, first, last)
                for c, kind, n, j in steps("SP", first, last):
                    if kind in ("OP", "T"):
                        load_after(kind, n, b, first, last)
                    elif kind == "ST":
                        db, tc = target(c)
                        stack(tc, b, db)
                    elif kind == "RC":
                        row_to_dram(n, b)

            all_batches(nc.sync, body)

        def tensor_program(pe, attention):
            def three(out_ap, a_hi, a_lo, b_hi, b_lo):
                last = None
                for i in range(NF):
                    for n, (a, m) in enumerate(((a_hi, b_hi), (a_lo, b_hi), (a_hi, b_lo))):
                        last = nc.tensor.matmul(out_ap, a(i), m(i), start=(i == 0 and n == 0),
                                                stop=(i == NF - 1 and n == 2))
                return last

            free = dict.fromkeys(range(NJB))

            def jb_free(j):
                if free[j] is not None:
                    wait(pe, *free[j])

            def jb_held(j, sem_, per, b, offset):
                free[j] = (sem_, per, b, offset)

            def item(kind, n, c, b, db=0, j=None):
                u4 = 4 * db + c
                if kind == "A":
                    if n < NT:
                        if n == 0:
                            wait(pe, s["max_rows_in"], 128, b, 32 * (u4 + 1))
                        for h2 in range(2):
                            wait(pe, s["exp_done"], 32, b, 8 * u4 + 2 * n + h2 - 1)
                            for h in (2 * h2, 2 * h2 + 1):
                                last = nc.tensor.matmul(
                                    sc[:, h, :], k_stack[c % 2][0:MAXROW + 2, h * S + n * P:h * S + (n + 1) * P],
                                    q_stack[c % 2][0:MAXROW + 2, h * S:(h + 1) * S], start=True, stop=True)
                            last.then_inc(s["st_done"], 1)
                    if n >= 1:
                        kt = n - 1
                        if kt == 0:
                            wait(pe, s["ou_done"], 4, b, u4)
                        if c == 0:
                            wait(pe, s["v_done"], NT, b, NT * db + kt + 1)
                        wait(pe, s["exp_done"], 32, b, 8 * u4 + 2 * kt + 2)
                        for h in range(HG):
                            last = nc.tensor.matmul(
                                hb[h * HD:(h + 1) * HD, :], values[:, kt, (HG * c + h) * HD:(HG * c + h + 1) * HD],
                                probs[:, kt % 2, h, :], start=(kt == 0), stop=(kt == NT - 1))
                        last.then_inc(s["pv_done"], 1)
                elif kind == "M":
                    g = u4 + 1
                    if n % NT == 0:
                        wait(pe, stacked[n // NT], 4 * 16 * 6, b, 16 * 6 * (g + 1))
                    jb_free(j)
                    h, st = n // NT, (c + 1) % 2
                    nc.tensor.matmul(jbs[j][:], q_stack[st][0:MAXROW, n * P:(n + 1) * P],
                                     k_stack[st][0:MAXROW, h * S:(h + 1) * S], start=True, stop=True)\
                        .then_inc(s["ms_done"], 1)
                    jb_held(j, s["mx_done"], 64, b, 16 * g + n + 1)
                elif kind == "MT":
                    wait(pe, s["mc_done"], 4, b, u4 + 2)
                    jb_free(j)
                    nc.tensor.transpose(jbs[j][0:32, 0:P], max_parts[:, :].bitcast(F32), ident[:]).then_inc(s["mt_mm"], 1)
                    jb_held(j, s["mt_copied"], 4, b, u4 + 2)
                elif kind == "SUM":
                    wait(pe, s["acc_done"], 24, b, 6 * (u4 - 1) + 6)
                    jb_free(j)
                    for h in range(HG):
                        last = nc.tensor.matmul(jbs[j][h * HD:(h + 1) * HD, :], ones[:], psum_keys[:, h, :],
                                                start=True, stop=True)
                    last.then_inc(s["sum_mm"], 1)
                    jb_held(j, s["sum_used"], 4, b, u4)
                elif kind == "SC":
                    wait(pe, s["sum_used"], 4, b, u4)
                    jb_free(j)
                    for k in range(NT):
                        last = nc.tensor.transpose(jbs[j][:, k * P:(k + 1) * P], sums[:, k * P:(k + 1) * P], ident[:])
                    last.then_inc(s["sc_mm"], 1)
                    jb_held(j, s["sc_used"], 4, b, u4)
                elif kind in ("NM", "NMP"):
                    g = late(kind, u4)
                    wait(pe, s["wide_done"], 4, b, g + 1)
                    jb_free(j)
                    for k in range(NT):
                        last = nc.tensor.transpose(jbs[j][:, k * P:(k + 1) * P], sums[:, k * P:(k + 1) * P], ident[:])
                    last.then_inc(s["nm_mm"], 1)
                    jb_held(j, s["nm_chain"], 4, b, g + 1)
                elif kind in ("Q", "K"):
                    i = 0 if kind == "Q" else 1
                    src_hi, src_lo = (xn_hi, xn_lo) if i == 0 else (c_hi, c_lo)
                    wait(pe, s["t_lo"], 8, b, 8 * (db + 1))
                    wait(pe, s["t_hi"], 8, b, 8 * (db + 1))
                    jb_free(j)
                    three(jbs[j][:], lambda k: w_hi[i][:, k, c * P:(c + 1) * P], lambda k: w_lo[i][:, k, c * P:(c + 1) * P],
                          lambda k: src_hi[:, k, :], lambda k: src_lo[:, k, :]).then_inc(s["qk_mm"], 1)
                    jb_held(j, s["lo_done"], 8, b, 2 * u4 + i + 1)
                elif kind == "V":
                    jb_free(j)
                    three(jbs[j][:], lambda k: c_hi[:, k, n * P:(n + 1) * P], lambda k: c_lo[:, k, n * P:(n + 1) * P],
                          lambda k: w_hi[2][:, k, :], lambda k: w_lo[2][:, k, :]).then_inc(s["v_mm"], 1)
                    jb_held(j, s["v_done"], NT, b, n + 1)
                elif kind == "OP":
                    wait(pe, s["nm_done"], 4, b, 0)
                    jb_free(j)
                    three(jbs[j][:], lambda k: heads_hi[:, k, n * P:(n + 1) * P], lambda k: heads_lo[:, k, n * P:(n + 1) * P],
                          lambda k: w_hi[3][:, k, :], lambda k: w_lo[3][:, k, :]).then_inc(s["op_mm"], 1)
                    jb_held(j, s["x1_done"], NT, b, -NT + n + 1)
                elif kind == "T":
                    name = ("C" if n < NT else "X") + str(n % NT)
                    if n < NT:
                        wait_staged_pe(name, b, db - 1)
                    else:
                        wait(pe, s["lx_done"], NT, b, NT * db + n - NT + 1)
                    jb_free(j)
                    for k in range(NF):
                        last = nc.tensor.transpose(jbs[j][:, k * P:(k + 1) * P],
                                                   stage[slot_of(name)][:, k * P:(k + 1) * P], ident[:])
                    last.then_inc(s["t_mm"], 1)
                    jb_held(j, s["t_lo"], 8, b, 8 * db + n + 1)
                elif kind == "RT":
                    wait(pe, s["lr_done"], NT, b, -NT + n + 1)
                    jb_free(j)
                    for k in range(NF):
                        last = nc.tensor.transpose(jbs[j][:, k * P:(k + 1) * P], x2[:, k * P:(k + 1) * P], ident[:])
                    last.then_inc(s["rt_mm"], 1)
                    jb_held(j, s["rt_done"], NT, b, -NT + n + 1)
                elif kind == "RL":
                    wait(pe, s["rt_done"], NT, b, -NT + n + 1)
                    jb_free(j)
                    for k in range(NF):
                        last = nc.tensor.matmul(jbs[j][k * HD:(k + 1) * HD, 0:P], rw_pad[:, k, :], x2_t[:, k, :],
                                                start=True, stop=True)
                    last.then_inc(s["rl_mm"], 1)
                    jb_held(j, s["rl_done"], NT, b, -NT + n + 1)
                elif kind == "RS":
                    wait(pe, s["rl_done"], NT, b, -NT + n + 1)
                    jb_free(j)
                    nc.tensor.matmul(jbs[j][:, 0:E], part[:], sel[:], start=True, stop=True).then_inc(s["rs_mm"], 1)
                    jb_held(j, s["rs_done"], NT, b, -NT + n + 1)
                elif kind == "RC":
                    wait(pe, s["oh_done"], NT, b, -NT + n + 1)
                    jb_free(j)
                    nc.tensor.matmul(jbs[j][:, 0:E], before[:], chosen[:], start=True, stop=True)
                    nc.tensor.matmul(jbs[j][:, E:2 * E], ones_b[:], chosen[:], start=True, stop=True).then_inc(s["rc_mm"], 1)
                    jb_held(j, s["rc_done"], NT, b, -NT + n + 1)

            def wait_staged_pe(name, b, db):
                n, k = load_count(name)
                wait(pe, staged[name], 16 * n, b, 16 * n * (db + 1) + 16 * (k + 1))

            if not attention:
                for kind, n, j in with_banks(EPILOGUE):
                    item(kind, n, 0, B, 0, j)
                return

            pe.wait_ge(s["p_const"], 2)
            pe.wait_ge(s["w_in"], 64)
            for n in range(4 * NF):
                i, k = n // NF, n % NF
                if n >= 4:
                    pe.wait_ge(s["w_lo_done"], n - 3)
                for o in range(NF):
                    last = nc.tensor.transpose(sc[:, n % 4, o * P:(o + 1) * P],
                                               nat[i][:, o, k * P:(k + 1) * P], ident[:])
                last.then_inc(s["w_mm"], 1)
            pe.wait_ge(s["w_lo_done"], 4 * NF)
            pe.wait_ge(s["p_init"], 2)
            pe.wait_ge(s["c_in1"], 16)

            for kind, n, j in with_banks(OPENING):
                item(kind, n, 0, 0, 0, j)
            for k in range(16):
                item("M", k, -1, 0, 0, k % NJB)
            for kind, n, j in with_banks(OPENING_2):
                item(kind, n, 1 if kind in ("Q", "K") else -1, 0, 0, j)

            def body(b, first=False, last=False):
                mt_bank = banks["MT", 0, 3]
                if not first:
                    free.update(dict.fromkeys(free))
                    free[mt_bank] = (s["mt_copied"], 4, b, 1)
                for c, kind, n, j in steps("PE", first, last):
                    if kind in ("Q", "K"):
                        db, tc = target(c)
                        item(kind, n, tc, b, db, j)
                    elif kind == "T":
                        item(kind, n, c, b, 1, j)
                    else:
                        item(kind, n, c, b, 0, j)
                if not last:
                    for j in range(NJB):
                        if j != mt_bank:
                            jb_free(j)

            all_batches(nc.tensor, body)
            for kind, n, j in with_banks(CLOSING):
                item(kind, n, 0, B, 0, j)

        def scalar_program(act, attention):
            def item(kind, n, c, b, db=0, j=None):
                u4 = 4 * db + c
                if kind == "A" and n < NT:
                    for h2 in range(2):
                        wait(act, s["st_done"], 32, b, 8 * u4 + 2 * n + h2 + 1)
                        wait(act, s["pv_done"], 16, b, 4 * u4 + n - 1)
                        wait(act, s["acc_done"], 24, b, 6 * u4 + (h2 + 1 if n >= 2 else 2 * n - 4 + h2 + 1))
                        nc.scalar.activation(probs[:, n % 2, 2 * h2:2 * h2 + 2, :], sc[:, 2 * h2:2 * h2 + 2, :],
                                             ACT.Exp, scale=SCALE).then_inc(s["exp_done"], 1)
                elif kind == "OU":
                    wait(act, s["pv_done"], 16, b, 4 * u4)
                    wait(act, s["nm_done"], 4, b, u4 - 1)
                    nc.scalar.activation(heads_raw[:], hb[:], ACT.Copy).then_inc(s["ou_done"], 1)
                elif kind == "SUM":
                    wait(act, s["sum_mm"], 4, b, u4)
                    wait(act, s["nm_mm"], 4, b, u4 - 1)
                    nc.scalar.activation(sums[:], jbs[j][:], ACT.Copy).then_inc(s["sum_used"], 1)
                elif kind == "SC":
                    wait(act, s["sc_used"], 4, b, u4)
                    nc.scalar.activation(sums[:, :].rearrange("p (k h d) -> p k h d", k=NT, h=HG),
                                         recip[:, :, :].unsqueeze(3).broadcast_to([P, NT, HG, HD]), ACT.Copy)\
                        .then_inc(s["wide_done"], 1)
                elif kind in ("NM", "NMP"):
                    g = late(kind, u4)
                    wait(act, s["nm_chain"], 4, b, g + 1)
                    if g % 4 == 0:
                        wait(act, s["op_mm"], NT, b, NT * (g // 4))
                    nc.scalar.activation(heads_hi[:, g % 4, :], heads_raw[:], ACT.Identity,
                                         bias=bias[:, 2, g % 4:g % 4 + 1]).then_inc(s["nm_hi"], 1)
                elif kind in ("Q", "K"):
                    i = 0 if kind == "Q" else 1
                    wait(act, s["qk_mm"], 8, b, 2 * u4 + i + 1)
                    for h in range(HG):
                        wait(act, stacked[h], 4 * 16 * 6, b, 16 * 6 * u4)
                    nc.scalar.activation(qk_hi[:, i, :], jbs[j][:], ACT.Identity,
                                         bias=bias[:, i, c:c + 1]).then_inc(s["hi_done"], 1)
                elif kind == "NX":
                    tile, st = stage[slot_of(f"X{n}")], st1[n % 2]
                    wait(act, s["lx_pow"], NT, b, NT * db + n + 1)
                    nc.scalar.activation(tile[:], tile[:], ACT.Identity, scale=st[:, 9:10], bias=st[:, 10:11])\
                        .then_inc(s["lx_done"], 1)
                elif kind == "T":
                    wait(act, s["t_mm"], 8, b, 8 * db + n + 1)
                    dst = (c_hi if n < NT else xn_hi)[:, :, (n % NT) * P:(n % NT + 1) * P]
                    nc.scalar.activation(dst, jbs[j][:, :].rearrange("p (k q) -> p k q", q=P), ACT.Copy)\
                        .then_inc(s["t_hi"], 1)
                elif kind == "V":
                    wait(act, s["v_mm"], NT, b, n + 1)
                    nc.scalar.activation(values[:, n, :], jbs[j][:], ACT.Copy).then_inc(s["v_done"], 1)
                elif kind == "MT":
                    wait(act, s["mt_mm"], 4, b, u4 + 2)
                    wait(act, s["max_rows_in"], 128, b, 32 * (u4 + 1))
                    nc.scalar.activation(max_rows[:], jbs[j][0:32, 0:P], ACT.Copy).then_inc(s["mt_copied"], 1)
                    wait(act, s["mt_copied"], 4, b, u4 + 2)
                    for j in range(2):
                        act.dma_start(q_stack[(c + 1) % 2][MAXROW + j:MAXROW + j + 1, :].bitcast(F32),
                                      max_rows[16 * j:16 * (j + 1), :].bitcast(F32)).then_inc(s["max_rows_in"], 16)
                elif kind == "W":
                    wait(act, s[f"ew_in{n % 2}"], 0, 0, 16 * (n // 2 + 1))
                    nc.scalar.activation(e_hi[:, n, :, :], raw[n % 2][:, :, :], ACT.Copy).then_inc(s["ew_hi"], 1)
                elif kind == "NR":
                    st = st2[n % 2]
                    wait(act, s["lr_pow"], NT, b, -NT + n + 1)
                    nc.scalar.activation(x2[:], row[n % 2][:, 0:D], ACT.Identity, scale=st[:, 9:10], bias=st[:, 10:11])\
                        .then_inc(s["lr_done"], 1)
                elif kind == "RT":
                    wait(act, s["rt_mm"], NT, b, -NT + n + 1)
                    nc.scalar.activation(x2_t[:, :, :], jbs[j][:, :].rearrange("p (k q) -> p k q", q=P), ACT.Copy)\
                        .then_inc(s["rt_done"], 1)
                elif kind == "RL":
                    wait(act, s["rl_mm"], NT, b, -NT + n + 1)
                    nc.scalar.activation(part[:], jbs[j][:, 0:P], ACT.Copy).then_inc(s["rl_done"], 1)
                elif kind == "RS":
                    wait(act, s["rs_done"], NT, b, -NT + n + 1)
                    nc.scalar.activation(rt[:, 8:16], rt[:, 0:8], ACT.Exp, bias=rt[:, 17:18],
                                         accum_out=rt[:, 18:19]).then_inc(s["rs_exp"], 1)

            if not attention:
                for kind, n, j in with_banks(EPILOGUE):
                    item(kind, n, 0, B, 0, j)
                return

            act.wait_ge(s["c_in0"], 16 * 5)
            nc.scalar.activation(tanh_g[:], g_all[:], ACT.Tanh).then_inc(s["a_const"], 1)
            for n in range(4 * NF):
                i, k = n // NF, n % NF
                act.wait_ge(s["w_mm"], n + 1)
                nc.scalar.activation(w_hi[i][:, k, :], sc[:, n % 4, :], ACT.Copy).then_inc(s["w_hi_done"], 1)

            for kind, n, j in with_banks(OPENING):
                item(kind, n, 0, 0, 0, j)
            for kind, n, j in with_banks(OPENING_2):
                item(kind, n, 1 if kind in ("Q", "K") else -1, 0, 0, j)

            def body(b, first=False, last=False):
                for c, kind, n, j in steps("ACT", first, last):
                    if kind in ("Q", "K"):
                        db, tc = target(c)
                        item(kind, n, tc, b, db, j)
                    elif kind in ("T", "NX"):
                        item(kind, n, c, b, 1, j)
                    else:
                        item(kind, n, c, b, 0, j)

            all_batches(nc.scalar, body)
            for kind, n, j in with_banks(CLOSING):
                item(kind, n, 0, B, 0, j)

        def vector_program(dve, attention):
            def chain(sem_, per, b, offset):
                k = [0]

                def link(ins, alone=None):
                    k[0] += 1
                    assert k[0] <= per[1]
                    ins.then_inc(sem_, 1)
                    wait(dve, sem_, per[0] * per[1], b, offset * per[1] + k[0], alone)
                return link

            def layernorm_stats(link, src, st):
                nc.vector.bn_stats(st[:, 0:6], src)
                nc.vector.drain()
                link(nc.vector.bn_aggr(st[:, 6:8], st[:, 0:6]))
                link(nc.vector.tensor_scalar(st[:, 11:12], st[:, 6:7], -1.0, None, ALU.mult))
                return nc.vector.tensor_scalar(st[:, 8:9], st[:, 7:8], EPS, None, ALU.add)

            def item(kind, n, c, b, db=0, j=None):
                u4 = 4 * db + c
                if kind == "M":
                    wait(dve, s["ms_done"], 64, b, 16 * (u4 + 1) + n + 1)
                    if n == 0:
                        wait(dve, s["mc_done"], 4, b, u4 + 1)
                    nc.vector.tensor_reduce(maxima[:, n:n + 1], jbs[j][:], AX.X, ALU.max).then_inc(s["mx_done"], 1)
                elif kind == "MC":
                    wait(dve, s["mx_done"], 64, b, 16 * (u4 + 2))
                    wait(dve, s["mt_mm"], 4, b, u4 + 1)
                    nc.vector.tensor_copy(max_parts[:, 0:16], maxima[:]).then_inc(s["mc_chain"], 1)
                    wait(dve, s["mc_chain"], 4, b, u4 + 2)
                    nc.vector.tensor_tensor(max_parts[:, 16:32], maxima[:], max_parts[:, 0:16].bitcast(F32),
                                            ALU.subtract).then_inc(s["mc_done"], 1)
                elif kind == "SC":
                    wait(dve, s["sc_mm"], 4, b, u4)
                    wait(dve, s["wide_done"], 4, b, u4 - 1)
                    nc.vector.reciprocal(recip[:, :, :], jbs[j][:, :].rearrange("p (k h d) -> p k h d", k=NT, h=HG)[:, :, :, 0])\
                        .then_inc(s["sc_used"], 1)
                elif kind in ("NM", "NMP"):
                    g = late(kind, u4)
                    wait(dve, s["ou_done"], 4, b, g + 1)
                    wait(dve, s["nm_mm"], 4, b, g + 1)
                    nc.vector.tensor_tensor(heads_raw[:], heads_raw[:], jbs[j][:], ALU.mult).then_inc(s["nm_chain"], 1)
                elif kind in ("NL", "NLP"):
                    g = late("NM" if kind == "NL" else "NMP", u4)
                    wait(dve, s["nm_hi"], 4, b, g + 1)
                    nc.vector.scalar_tensor_tensor(heads_lo[:, g % 4, :], heads_raw[:], bias[:, 2, g % 4:g % 4 + 1],
                                                   heads_hi[:, g % 4, :].bitcast(F32), ALU.add, ALU.subtract)\
                        .then_inc(s["nm_done"], 1)
                elif kind == "W":
                    dve.wait_ge(s["ew_hi"], n + 1)
                    nc.vector.tensor_tensor(e_lo[:, n, :, :], raw[n % 2][:, :, :], e_hi[:, n, :, :].bitcast(F32),
                                            ALU.subtract).then_inc(s["ew_lo"], 1)
                elif kind in ("Q", "K"):
                    i = 0 if kind == "Q" else 1
                    wait(dve, s["hi_done"], 8, b, 2 * u4 + i + 1)
                    nc.vector.scalar_tensor_tensor(qk_lo[:, i, :], jbs[j][:], bias[:, i, c:c + 1],
                                                   qk_hi[:, i, :].bitcast(F32), ALU.add, ALU.subtract)\
                        .then_inc(s["lo_done"], 1)
                elif kind == "LX":
                    name, link = f"X{n}", chain(s["lx_chain"], (NT, 2), b, NT * db + n)
                    m, k = load_count(name)
                    wait(dve, staged[name], 16 * m, b, 16 * m * db + 16 * (k + 1))
                    wait(dve, s["lx_done"], NT, b, NT * db + n - 1)
                    layernorm_stats(link, stage[slot_of(name)][:], st1[n % 2]).then_inc(s["lx_var"], 1)
                elif kind == "T":
                    hi, lo = (c_hi, c_lo) if n < NT else (xn_hi, xn_lo)
                    wait(dve, s["t_hi"], 8, b, 8 * db + n + 1)
                    cols = slice((n % NT) * P, (n % NT + 1) * P)
                    nc.vector.tensor_tensor(lo[:, :, cols], jbs[j][:, :].rearrange("p (k q) -> p k q", q=P),
                                            hi[:, :, cols].bitcast(F32), ALU.subtract).then_inc(s["t_lo"], 1)
                elif kind == "OP":
                    name = f"R{n}"
                    wait(dve, s["op_mm"], NT, b, -NT + n + 1)
                    wait(dve, s["xb_done"], NT, b, -NT + n + 1)
                    wait(dve, s[f"row_out{n % 2}"], 32, b, -32 + 16 * (n // 2) + 16)
                    nc.vector.scalar_tensor_tensor(row[n % 2][:, 0:D], jbs[j][:], tanh_g[:, 0:1], stage[slot_of(name)][:],
                                                   ALU.mult, ALU.add).then_inc(s["x1_done"], 1)
                elif kind == "LR":
                    link = chain(s["lr_chain"], (NT, 2), b, n - NT)
                    wait(dve, s["x1_done"], NT, b, -NT + n + 1)
                    r = row[n % 2]
                    layernorm_stats(link, r[:, 0:D], st2[n % 2]).then_inc(s["lr_var"], 1)
                elif kind == "RT":
                    wait(dve, s["lr_pow"], NT, b, -NT + n + 1)
                    nc.vector.tensor_copy(row[n % 2][:, D:D + 2], st2[n % 2][:, 9:11]).then_inc(s["rt_stats"], 1)
                elif kind == "RS":
                    link = chain(s["rs_chain"], (NT, 6), b, n - NT)
                    wait(dve, s["rs_mm"], NT, b, -NT + n + 1)
                    link(nc.vector.tensor_tensor(rt[:, 0:8], jbs[j][:, 0:E], rb_all[:], ALU.add))
                    link(nc.vector.tensor_reduce(rt[:, 16:17], rt[:, 0:8], AX.X, ALU.max))
                    nc.vector.tensor_scalar(rt[:, 17:18], rt[:, 16:17], -1.0, None, ALU.mult).then_inc(s["rs_done"], 1)
                    link(nc.vector.tensor_scalar(rt[:, 24:32], rt[:, 0:8], rt[:, 16:17], float(-E), ALU.is_equal, ALU.mult))
                    link(nc.vector.tensor_tensor(rt[:, 32:40], rt[:, 24:32], numbers[:], ALU.add))
                    link(nc.vector.tensor_reduce(rt[:, 20:21], rt[:, 32:40], AX.X, ALU.min))
                    link(nc.vector.tensor_scalar(rt[:, 40:48], rt[:, 32:40], rt[:, 20:21], None, ALU.is_equal))
                    nc.vector.tensor_copy(chosen[:], rt[:, 40:48]).then_inc(s["oh_done"], 1)
                elif kind == "RG":
                    link = chain(s["rg_chain"], (NT, 2), b, n - NT)
                    wait(dve, s["rs_exp"], NT, b, -NT + n + 1)
                    link(nc.vector.reciprocal(rt[:, 21:22], rt[:, 18:19]))
                    link(nc.vector.tensor_scalar(row[n % 2][:, D + 2:D + 3], rt[:, 21:22], tanh_g[:, 1:2], None, ALU.mult))
                elif kind == "RC":
                    link = chain(s["rc_chain"], (NT, 6), b, n - NT)
                    wait(dve, s["rc_mm"], NT, b, -NT + n + 1)
                    link(nc.vector.tensor_tensor(rt[:, 48:56], jbs[j][:, 0:E], counts[:], ALU.add))
                    link(nc.vector.tensor_tensor(rt[:, 56:64], rt[:, 48:56], rt[:, 40:48], ALU.mult))
                    link(nc.vector.tensor_tensor(counts[:], jbs[j][:, E:2 * E], counts[:], ALU.add))
                    link(nc.vector.reduce_sum(rt[:, 64:65], rt[:, 56:64], axis=AX.X))
                    wait(dve, s[f"listed{n % 2}"], 32, b, -32 + 16 * (n // 2) + 16)
                    link(nc.vector.tensor_copy(token_of[n % 2][:], token[:]))
                    link(nc.vector.tensor_scalar(token[:], token[:], float(P), None, ALU.add))
                    nc.vector.tensor_copy(dest[n % 2][:], rt[:, 64:65]).then_inc(s["rc_done"], 1)

            if not attention:
                for kind, n, j in with_banks(EPILOGUE):
                    item(kind, n, 0, B, 0, j)
                return

            dve.sem_inc(s["began"], 1)
            nc.vector.memset(rw_pad[:], 0.0).then_inc(s["d_const"], 1)
            nc.vector.memset(ones[:], 1.0).then_inc(s["d_const"], 1)
            nc.vector.memset(ones_b[:], 1.0).then_inc(s["d_const"], 1)
            for i in range(2):
                nc.vector.memset(k_stack[i][MAXROW:P, :].bitcast(F32), -1.0).then_inc(s["d_const"], 1)
            dve.wait_ge(s["a_const"], 1)
            dve.wait_ge(s["row_out0"], 16)
            dve.wait_ge(s["row_out1"], 16)
            dve.wait_ge(s["listed0"], 16)
            dve.wait_ge(s["listed1"], 16)
            nc.vector.tensor_scalar(gbo[:], gbo[:], tanh_g[:, 0:1], None, ALU.mult).then_inc(s["p_init"], 1)
            for n in range(4 * NF):
                i, k = n // NF, n % NF
                dve.wait_ge(s["w_hi_done"], n + 1)
                nc.vector.tensor_tensor(w_lo[i][:, k, :], sc[:, n % 4, :], w_hi[i][:, k, :].bitcast(F32),
                                        ALU.subtract).then_inc(s["w_lo_done"], 1)
            dve.wait_ge(s["p_const"], 5)

            for kind, n, j in with_banks(OPENING):
                item(kind, n, 0, 0, 0, j)
            for k in range(16):
                item("M", k, -1, 0, 0, k % NJB)
            for kind, n, j in with_banks(OPENING_2):
                item(kind, n, 1 if kind in ("Q", "K") else -1, 0, 0, j)

            def body(b, first=False, last=False):
                for c, kind, n, j in steps("DVE", first, last):
                    if kind in ("Q", "K"):
                        db, tc = target(c)
                        item(kind, n, tc, b, db, j)
                    elif kind in ("T", "LX"):
                        item(kind, n, c, b, 1, j)
                    else:
                        item(kind, n, c, b, 0, j)

            all_batches(nc.vector, body)
            for kind, n, j in with_banks(CLOSING):
                item(kind, n, 0, B, 0, j)

        def gpsimd_program(pool, attention):
            def item(kind, n, c, b, db=0, j=None):
                u4 = 4 * db + c
                if kind == "A" and 1 <= n < NT:
                    for h2 in range(2):
                        two = slice(2 * h2, 2 * h2 + 2)
                        wait(pool, s["exp_done"], 32, b, 8 * u4 + 2 * n + h2 + 1, s["began"])
                        if n == 1:
                            wait(pool, s["sum_mm"], 4, b, u4, s["began"])
                            in0 = probs[:, 0, two, :]
                        else:
                            wait(pool, s["acc_done"], 24, b, 6 * u4 + 2 * (n - 2) + h2 + 1, s["began"])
                            in0 = psum_keys[:, two, :]
                        nc.gpsimd.tensor_tensor(psum_keys[:, two, :], in0, probs[:, n % 2, two, :], ALU.add)\
                            .then_inc(s["acc_done"], 1)
                elif kind == "LX":
                    wait(pool, s["lx_var"], NT, b, NT * db + n + 1, s["began"])
                    st = st1[n % 2]
                    nc.gpsimd.tensor_tensor(st[:, 9:10], st[:, 8:9], minus_half[:], ALU.pow).then_inc(s["lx_rstd"], 1)
                    wait(pool, s["lx_rstd"], NT, b, NT * db + n + 1, s["began"])
                    nc.gpsimd.tensor_tensor(st[:, 10:11], st[:, 9:10], st[:, 11:12], ALU.mult).then_inc(s["lx_pow"], 1)
                elif kind == "LR":
                    wait(pool, s["lr_var"], NT, b, -NT + n + 1, s["began"])
                    st = st2[n % 2]
                    nc.gpsimd.tensor_tensor(st[:, 9:10], st[:, 8:9], minus_half[:], ALU.pow).then_inc(s["lr_rstd"], 1)
                    wait(pool, s["lr_rstd"], NT, b, -NT + n + 1, s["began"])
                    nc.gpsimd.tensor_tensor(st[:, 10:11], st[:, 9:10], st[:, 11:12], ALU.mult).then_inc(s["lr_pow"], 1)
                elif kind == "OP":
                    name = f"R{n}"
                    m, k = load_count(name)
                    wait(pool, staged[name], 16 * m, b, -16 * m + 16 * (k + 1), s["began"])
                    tile = stage[slot_of(name)]
                    nc.gpsimd.tensor_tensor(tile[:], tile[:], gbo[:], ALU.add).then_inc(s["xb_done"], 1)
                elif kind == "RC":
                    wait(pool, s["rc_done"], NT, b, -NT + n + 1, s["began"])
                    nc.gpsimd.indirect_dma_start(
                        out=lists_dram[:, :], out_offset=bass.IndirectOffsetOnAxis(ap=dest[n % 2][:, 0:1].bitcast(U32), axis=0),
                        in_=token_of[n % 2][:, :], in_offset=None).then_inc(s[f"listed{n % 2}"], 16)

            if not attention:
                for kind, n, j in with_banks(EPILOGUE):
                    item(kind, n, 0, B)
                for j in range(2):
                    pool.wait_ge(s[f"listed{j}"], 16 + 32 * B)
                return

            empty = x2[:, 0:E * TOKENS // P]
            nc.gpsimd.memset(empty, float(TOKENS)).then_inc(s["empty"], 1)
            pool.wait_ge(s["empty"], 1)
            halves = lists_dram.rearrange("(h p f) a -> h p (f a)", h=2, p=P)
            for j in range(2):
                pool.dma_start(halves[j], empty[:, 0:E * TOKENS // P // 2]).then_inc(s[f"listed{j}"], 16)
            nc.gpsimd.memset(ident[:], 0.0).then_inc(s["p_const"], 1)
            pool.wait_ge(s["p_const"], 1)
            nc.gpsimd.affine_select(out=ident[:], in_=ident[:], compare_op=ALU.not_equal, fill=1.0, base=0,
                                    pattern=[[-1, P]], channel_multiplier=1).then_inc(s["p_const"], 1)
            nc.gpsimd.iota(numbers[:], [[1, E]], base=0, channel_multiplier=0,
                           allow_small_or_imprecise_dtypes=True).then_inc(s["p_const"], 1)
            nc.gpsimd.iota(token[:], [[0, 1]], base=0, channel_multiplier=1,
                           allow_small_or_imprecise_dtypes=True).then_inc(s["p_const"], 1)
            nc.gpsimd.iota(counts[:], [[TOKENS, E]], base=0, channel_multiplier=0,
                           allow_small_or_imprecise_dtypes=True).then_inc(s["p_const"], 1)
            nc.gpsimd.memset(minus_half[:], -0.5).then_inc(s["p_const"], 1)
            nc.gpsimd.memset(sel[:], 0.0).then_inc(s["p_const"], 1)
            pool.wait_ge(s["p_const"], 7)
            for k in range(NF):
                nc.gpsimd.affine_select(out=sel[:], in_=sel[:], compare_op=ALU.not_equal, fill=1.0, base=-k * HD,
                                        pattern=[[-1, E]], channel_multiplier=1).then_inc(s["p_const"], 1)
                pool.wait_ge(s["p_const"], 8 + k)
            nc.gpsimd.memset(before[:], 1.0).then_inc(s["p_const"], 1)
            pool.wait_ge(s["p_const"], 12)
            nc.gpsimd.affine_select(out=before[:], in_=before[:], compare_op=ALU.is_gt, fill=0.0, base=0,
                                    pattern=[[1, P]], channel_multiplier=-1).then_inc(s["p_init"], 1)

            pool.wait_ge(s["p_const"], 12)
            for kind, n, j in with_banks(OPENING):
                item(kind, n, 0, 0)
            pool.wait_ge(s["p_init"], 2)

            def body(b, first=False, last=False):
                for c, kind, n, j in steps("POOL", first, last):
                    item(kind, n, c, b, 1 if kind == "LX" else 0)

            all_batches(nc.gpsimd, body)

        with nc.Block() as block:
            block.sync(lambda eng: sync_program(eng, True))
            block.tensor(lambda eng: tensor_program(eng, True))
            block.scalar(lambda eng: scalar_program(eng, True))
            block.vector(lambda eng: vector_program(eng, True))
            block.gpsimd(lambda eng: gpsimd_program(eng, True))
        attention_only.close()
        e_hi = kept("e_hi", [P, E, NF, D], F32R)
        e_lo = kept("e_lo", [P, E, NF, D], F32R)
        with nc.sbuf_tensor("raw0", [P, NF, D], F32) as raw0, nc.sbuf_tensor("raw1", [P, NF, D], F32) as raw1, \
                nc.Block() as block:
            raw = [raw0, raw1]
            block.sync(lambda eng: sync_program(eng, False))
            block.tensor(lambda eng: tensor_program(eng, False))
            block.scalar(lambda eng: scalar_program(eng, False))
            block.vector(lambda eng: vector_program(eng, False))
            block.gpsimd(lambda eng: gpsimd_program(eng, False))
        return dict(e_hi=e_hi, e_lo=e_lo, row=row, stage=stage, x2=x2, heads_hi=heads_hi, heads_lo=heads_lo)


def expert_part(nc, kept_tiles, eb, rows_dram, lists_dram, counts, ident, out_rows):
    with ExitStack() as es:
        def sb(name, shape, dt=F32):
            return es.enter_context(nc.sbuf_tensor(name, shape, dt))

        def ps(name, shape):
            return es.enter_context(nc.psum_tensor(name, shape, F32))

        def sem(name):
            return es.enter_context(nc.semaphore("e_" + name))

        e_hi, e_lo = kept_tiles["e_hi"], kept_tiles["e_lo"]
        xt_hi = [kept_tiles["heads_hi"][:, :, i * P:(i + 1) * P] for i in range(SLOTS)]
        xt_lo = [kept_tiles["heads_lo"][:, :, i * P:(i + 1) * P] for i in range(SLOTS)]
        got = kept_tiles["row"] + [sb(f"got{i}", [P, ROW]) for i in range(2, SLOTS)]
        done = kept_tiles["stage"] + [kept_tiles["x2"]]
        xe = [sb(f"xe{i}", [P, D]) for i in range(2)]
        eb_all = sb("eb_all", [P, E, D])
        small = sb("small", [P, 6, E])
        plan = sb("plan", [P, 8])
        one = sb("one", [P, E])
        tiles_i = sb("tiles_i", [P, E], I32)
        number = sb("number", [P, E])
        lane = sb("lane", [P, 1])
        spare = sb("spare", [P, 1])
        list_row = sb("list_row", [P, 1], I32)
        tokens = sb("tokens", [P, P])
        expert_i = sb("expert_i", [1, P], I32)
        src_i = sb("src_i", [P, TILES], I32)
        dst_i = sb("dst_i", [P, TILES], I32)
        index = [sb(f"index{i}", [P, 1], I32) for i in range(SLOTS)]
        target = [sb(f"target{i}", [P, 1], I32) for i in range(SLOTS)]
        tp = [ps(f"tp{i}", [P, NF * P]) for i in range(2)]
        yb = [ps(f"yb{i}", [P, D]) for i in range(SLOTS)]

        s = {n: sem(n) for n in ("eb_in", "const", "chain", "src_ready", "plan_ready", "xe", "tp", "hi", "lo", "y",
                                 "row_ready", "tokens_in", "tokens_ok", "plan_mm", "y1", "fin",
                                 "paced")
             + tuple(f"in{i}" for i in range(SLOTS)) + tuple(f"out{i}" for i in range(SLOTS))}
        block = es.enter_context(nc.Block())
        TURNS = TILES // SLOTS

        def at(eng, sem_, turn, j, t_off=0):
            if isinstance(turn, int):
                t = SLOTS * turn + j + t_off
                if 0 <= t < TILES:
                    eng.wait_ge(sem_, t + 1)
            else:
                eng.wait_ge(sem_, turn * SLOTS + (j + t_off + 1))

        def at_dma(eng, name, turn, j, t_off=0):
            slot, back = (j + t_off) % SLOTS, (j + t_off) // SLOTS
            if isinstance(turn, int):
                if turn + back >= 0:
                    eng.wait_ge(s[f"{name}{slot}"], 16 * (turn + back + 1))
            else:
                eng.wait_ge(s[f"{name}{slot}"], turn * 16 + 16 * (back + 1))

        def exists(turn, j, t_off):
            return not isinstance(turn, int) or 0 <= SLOTS * turn + j + t_off < TILES

        def run(engine, body):
            for j in range(SLOTS):
                body(0, j)
            with engine.Fori(1, TURNS - 1) as turn:
                for j in range(SLOTS):
                    body(turn, j)
            for j in range(SLOTS):
                body(TURNS - 1, j)

        @block.sync
        def _(sp):
            sp.dma_start(eb_all[:, :, :], eb.partition_broadcast(P)).then_inc(s["eb_in"], 16)

        @block.scalar
        def _(act):
            def normalise(turn, j, ahead):
                if exists(turn, j, ahead):
                    slot = (j + ahead) % SLOTS
                    g = got[slot]
                    at_dma(act, "in", turn, j, ahead)
                    at(act, s["tp"], turn, j, ahead - 2)
                    nc.scalar.activation(xe[slot % 2][:], g[:, 0:D], ACT.Identity, scale=g[:, D:D + 1],
                                         bias=g[:, D + 1:D + 2]).then_inc(s["xe"], 1)

            def high(turn, j, ahead):
                if exists(turn, j, ahead):
                    slot = (j + ahead) % SLOTS
                    at(act, s["tp"], turn, j, ahead)
                    at(act, s["y"], turn, j, ahead - SLOTS)
                    nc.scalar.activation(xt_hi[slot], tp[slot % 2][:, :].rearrange("p (k q) -> p k q", q=P), ACT.Copy)\
                        .then_inc(s["hi"], 1)

            normalise(0, 0, 0)
            high(0, 0, 0)
            normalise(0, 0, 1)

            def body(turn, j):
                high(turn, j, 1)
                normalise(turn, j, 2)
            run(nc.scalar, body)

        @block.vector
        def _(dve):
            k = [0]

            def link(ins):
                k[0] += 1
                ins.then_inc(s["chain"], 1)
                dve.wait_ge(s["chain"], k[0])

            dve.wait_ge(s["const"], 2)
            cnt, ntl, end, tmp, past, past_tiles = (small[:, i, :] for i in range(6))
            link(nc.vector.memset(one[:], 1.0))
            link(nc.vector.scalar_tensor_tensor(cnt, number[:], float(-TOKENS), counts[:], ALU.mult, ALU.add))
            link(nc.vector.tensor_scalar(tmp, cnt, 1.0 / P, (P - 1.0) / P - (P - 1.0) / (2 * P), ALU.mult, ALU.add))
            link(nc.vector.tensor_copy(tiles_i[:], tmp))
            link(nc.vector.tensor_copy(ntl, tiles_i[:]))
            link(nc.vector.tensor_tensor_scan(end, one[:], ntl, 0.0, ALU.mult, ALU.add))
            tile, expert, start, bad, in_list, t1 = (plan[:, i:i + 1] for i in range(6))
            link(nc.vector.tensor_scalar(t1, lane[:], 1.0, end[:, E - 1:E], ALU.add, ALU.min))
            link(nc.vector.tensor_scalar(tile, t1, 1.0, None, ALU.subtract))
            link(nc.vector.tensor_scalar(past, end, tile, None, ALU.is_le))
            link(nc.vector.reduce_sum(expert, past, axis=AX.X))
            link(nc.vector.tensor_tensor(past_tiles, past, ntl, ALU.mult))
            link(nc.vector.reduce_sum(start, past_tiles, axis=AX.X))
            link(nc.vector.tensor_tensor(in_list, tile, start, ALU.subtract))
            link(nc.vector.scalar_tensor_tensor(in_list, expert, float(TOKENS // P), in_list, ALU.mult, ALU.add))
            nc.vector.tensor_copy(list_row[:], in_list).then_inc(s["row_ready"], 1)
            link(nc.vector.tensor_tensor(bad, lane[:], tile, ALU.is_gt))
            link(nc.vector.tensor_scalar(bad, bad, float(2 * TOKENS), None, ALU.mult))
            dve.wait_ge(s["tokens_in"], 16)
            nc.vector.tensor_scalar(tokens[:], tokens[:], bad, None, ALU.add).then_inc(s["tokens_ok"], 1)
            dve.wait_ge(s["plan_mm"], 1)
            nc.vector.tensor_scalar(src_i[:], tp[0][:, 0:TILES], float(TOKENS - 1), None, ALU.min).then_inc(s["src_ready"], 1)
            dve.wait_ge(s["src_ready"], 1)
            for i in range(SLOTS):
                nc.vector.tensor_copy(index[i][:], src_i[:, i:i + 1])
            nc.vector.tensor_copy(dst_i[:], tp[0][:, 0:TILES]).then_inc(s["plan_ready"], 1)
            nc.vector.tensor_copy(expert_i[:], tp[1][0:1, 0:P]).then_inc(s["plan_ready"], 1)
            dve.wait_ge(s["eb_in"], 16)
            dve.wait_ge(s["plan_ready"], 2)

            def low(turn, j, ahead):
                if exists(turn, j, ahead):
                    slot = (j + ahead) % SLOTS
                    at(dve, s["hi"], turn, j, ahead)
                    nc.vector.tensor_tensor(xt_lo[slot], tp[slot % 2][:, :].rearrange("p (k q) -> p k q", q=P),
                                            xt_hi[slot].bitcast(F32), ALU.subtract).then_inc(s["lo"], 1)

            def body(turn, j):
                t = SLOTS * turn + j
                low(turn, j, 1)
                e = nc.vector.value_load(expert_i[0:1, bass.ds(t, 1)], min_val=0, max_val=E - 1)
                g = got[j]
                at_dma(dve, "out", turn, j, -SLOTS)
                if exists(turn, j, SLOTS):
                    at_dma(dve, "in", turn, j)
                    nc.vector.tensor_copy(index[j][:], src_i[:, bass.ds(t + SLOTS, 1)])
                nc.vector.tensor_copy(target[j][:], dst_i[:, bass.ds(t, 1)])
                at(dve, s["y"], turn, j)
                nc.vector.tensor_tensor(done[j][:], yb[j][:], eb_all[:, bass.ds(e, 1), :].rearrange("p a d -> p (a d)"),
                                        ALU.add).then_inc(s["y1"], 1)
                at(dve, s["y1"], turn, j)
                nc.vector.scalar_tensor_tensor(done[j][:], done[j][:], g[:, D + 2:D + 3], g[:, 0:D], ALU.mult, ALU.add)\
                    .then_inc(s["fin"], 1)

            low(0, 0, 0)
            run(nc.vector, body)

        @block.tensor
        def _(pe):
            pe.wait_ge(s["tokens_ok"], 1)
            nc.tensor.transpose(tp[0][:, 0:P], tokens[:], ident[:])
            nc.tensor.transpose(tp[1][0:1, 0:P], plan[:, 1:2], ident[:]).then_inc(s["plan_mm"], 1)
            pe.wait_ge(s["plan_ready"], 2)
            pe.wait_ge(s["src_ready"], 1)

            def turn_over(turn, j, ahead):
                if exists(turn, j, ahead):
                    slot = (j + ahead) % SLOTS
                    at(pe, s["xe"], turn, j, ahead)
                    at(pe, s["lo"], turn, j, ahead - 2)
                    for i in range(NF):
                        last = nc.tensor.transpose(tp[slot % 2][:, i * P:(i + 1) * P],
                                                   xe[slot % 2][:, i * P:(i + 1) * P], ident[:])
                    last.then_inc(s["tp"], 1)

            def body(turn, j):
                turn_over(turn, j, 1)
                e = nc.tensor.value_load(expert_i[0:1, bass.ds(SLOTS * turn + j, 1)], min_val=0, max_val=E - 1)
                at(pe, s["hi"], turn, j)
                at(pe, s["lo"], turn, j)
                at(pe, s["y1"], turn, j, -SLOTS)
                for i in range(NF):
                    for n, (a, w) in enumerate(((xt_hi, e_hi), (xt_lo, e_hi), (xt_hi, e_lo))):
                        last = nc.tensor.matmul(yb[j][:], a[j][:, i, :],
                                                w[:, bass.ds(e, 1), i, :].rearrange("p a d -> p (a d)"),
                                                start=(i == 0 and n == 0), stop=(i == NF - 1 and n == 2))
                last.then_inc(s["y"], 1)

            turn_over(0, 0, 0)
            run(nc.tensor, body)

        @block.gpsimd
        def _(pool):
            nc.gpsimd.iota(number[:], [[1, E]], base=0, channel_multiplier=0,
                           allow_small_or_imprecise_dtypes=True).then_inc(s["const"], 1)
            nc.gpsimd.iota(lane[:], [[0, 1]], base=0, channel_multiplier=1,
                           allow_small_or_imprecise_dtypes=True).then_inc(s["const"], 1)
            pool.wait_ge(s["row_ready"], 1)
            lists = lists_dram.rearrange("(r q) a -> r (q a)", q=P)
            nc.gpsimd.indirect_dma_start(
                out=tokens[:, :], out_offset=None, in_=lists,
                in_offset=bass.IndirectOffsetOnAxis(ap=list_row[:, 0:1].bitcast(U32), axis=0)).then_inc(s["tokens_in"], 16)

            def gather(turn, j, ahead):
                if exists(turn, j, ahead):
                    slot = (j + ahead) % SLOTS
                    nc.gpsimd.indirect_dma_start(
                        out=got[slot][:, :], out_offset=None, in_=rows_dram[:, :],
                        in_offset=bass.IndirectOffsetOnAxis(ap=index[slot][:, 0:1].bitcast(U32), axis=0))\
                        .then_inc(s[f"in{slot}"], 16)

            def send(turn, j, back):
                slot = (j - back) % SLOTS
                nc.gpsimd.indirect_dma_start(
                    out=out_rows[:, :],
                    out_offset=bass.IndirectOffsetOnAxis(ap=target[slot][:, 0:1].bitcast(U32), axis=0),
                    in_=done[slot][:, :], in_offset=None, bounds_check=TOKENS - 1, oob_is_err=False)\
                    .then_inc(s[f"out{slot}"], 16)

            pool.wait_ge(s["plan_ready"], 2)
            for i in range(SLOTS - 1):
                gather(0, i, 0)

            def body(turn, j):
                if exists(turn, j, -1):
                    at(pool, s["paced"], turn, j, -2)
                    at(pool, s["fin"], turn, j, -1)
                    nc.gpsimd.tensor_tensor(spare[:], lane[:], lane[:], ALU.add).then_inc(s["paced"], 1)
                    send(turn, j, 1)
                gather(turn, j, SLOTS - 1)
            run(nc.gpsimd, body)
            pool.wait_ge(s["fin"], TILES)
            send(TURNS, 0, 1)
            for j in range(SLOTS):
                pool.wait_ge(s[f"out{j}"], 16 * TURNS)


_INS = ["x", "ctx_1024", "g_xattn", "g_ffn", "L0_xattn_Wq", "L0_xattn_bq", "L0_xattn_Wk", "L0_xattn_bk",
        "L0_xattn_Wv", "L0_xattn_bv", "L0_xattn_Wo", "L0_xattn_bo", "L0_ffn_router_w", "L0_ffn_router_b",
        "L0_ffn_expert_w", "L0_ffn_expert_b"]


def kernel(**inputs):
    import numpy as np
    import concourse.bacc as bacc
    from concourse.bass_utils import run_bass_kernel_spmd

    nc = bacc.Bacc("TRN2", target_bir_lowering=False, num_devices=1)
    arrays, args = {}, []
    for name in _INS:
        a = np.ascontiguousarray(inputs[name])
        arrays[f"in_{name}"] = a
        args.append(nc.dram_tensor(f"in_{name}", a.shape, mybir.dt.from_np(a.dtype), kind="ExternalInput").ap())
    out = nc.dram_tensor("out_x", [B, S, D], F32, kind="ExternalOutput").ap()
    build(nc, *args, out)
    r = run_bass_kernel_spmd(nc, [arrays], core_ids=[0])
    return r.results[0]["out_x"]
```
